# Optimizing a Trainium2 kernel written in Bass

```python
import numpy as np
import jax
import jax.numpy as jnp

def _softmax(x, axis=-1):
    return jax.nn.softmax(x, axis=axis)

def _gelu(x):
    return jax.nn.gelu(x, approximate=True)

def _silu(x):
    return jax.nn.silu(x)

def _sigmoid(x):
    return jax.nn.sigmoid(x)

def _layernorm(x, axis=-1, eps=1e-05):
    m = jnp.mean(x, axis=axis, keepdims=True)
    v = jnp.var(x, axis=axis, keepdims=True)
    return (x - m) / jnp.sqrt(v + eps)

def _scatter_add(tgt, idx, src, axis=0):
    return tgt.at[idx].add(src)

def _segment_sum(src, seg, n):
    return jax.ops.segment_sum(src, seg, n)
kernel_name = 'mk_prb_d1_jaxref_r8_21286a'

def setup_inputs(seed: int=0):
    np.random.seed(seed)
    _w = jnp.asarray

    def _L0_attn_setup():
        import jax, jax.numpy as jnp
        import numpy as np
        import math
        N_HEAD = 16
        N_EMBD = 128
        HEAD_DIM = N_EMBD // N_HEAD
        ROPE_BASE = 10000.0

        def _rope_cos_sin(T, dh, dtype):
            inv_freq = 1.0 / ROPE_BASE ** (jnp.arange(0, dh, 2, dtype=jnp.float32) / dh)
            freqs = jnp.arange(T, dtype=jnp.float32)[:, None] * inv_freq[None, :]
            cos = jnp.repeat(jnp.cos(freqs), 2, axis=-1).astype(dtype)
            sin = jnp.repeat(jnp.sin(freqs), 2, axis=-1).astype(dtype)
            return (cos, sin)

        def _apply_rope(x, cos, sin):
            x_even = x[..., ::2]
            x_odd = x[..., 1::2]
            x_rot = jnp.stack((-x_odd, x_even), axis=-1).reshape(x.shape)
            return x * cos + x_rot * sin
        key = jax.random.key(seed)
        k1, k2, k3 = jax.random.split(key, 3)
        B, T, C = (2, 256, N_EMBD)
        x = jax.random.normal(k1, (B, T, C), dtype=jnp.float32)
        Wqkv = jax.random.normal(k2, (C, 3 * C), dtype=jnp.float32) * (1.0 / math.sqrt(C))
        Wproj = jax.random.normal(k3, (C, C), dtype=jnp.float32) * (1.0 / math.sqrt(C))
        return {'x': x, 'Wqkv': Wqkv, 'Wproj': Wproj}
    _L0_attn_in = _L0_attn_setup()

    def _L0_ffn_setup():
        import jax, jax.numpy as jnp
        import numpy as np
        B, T, D = (2, 256, 128)
        DCD = 512
        RET = 128
        NEXP = 512
        NKEYS = 64
        H = 4
        KPH = 8
        key = jax.random.key(seed)
        ks = jax.random.split(key, 10)
        s = lambda k, shape, scale: jax.random.normal(k, shape, jnp.float32) * scale
        return {'hidden_states': jax.random.normal(ks[0], (B, T, D), jnp.float32), 'Wg': s(ks[1], (D, DCD), 0.02), 'bg': jnp.zeros((DCD,), jnp.float32), 'Wu': s(ks[2], (D, DCD), 0.02), 'bu': jnp.zeros((DCD,), jnp.float32), 'Wd': s(ks[3], (DCD, D), 0.02), 'bd': jnp.zeros((D,), jnp.float32), 'Wq': s(ks[4], (D, RET * H), 0.02), 'keys': s(ks[5], (H, NKEYS, 2, RET // 2), 0.02), 'down_embed': s(ks[6], (NEXP, D), 0.02), 'up_embed': s(ks[7], (NEXP, D), 0.02)}
    _L0_ffn_in = _L0_ffn_setup()
    _d = {'L0_attn_x': _L0_attn_in['x'], 'L0_attn_Wqkv': _L0_attn_in['Wqkv'], 'L0_attn_Wproj': _L0_attn_in['Wproj'], 'L0_ffn_Wg': _L0_ffn_in['Wg'], 'L0_ffn_bg': _L0_ffn_in['bg'], 'L0_ffn_Wu': _L0_ffn_in['Wu'], 'L0_ffn_bu': _L0_ffn_in['bu'], 'L0_ffn_Wd': _L0_ffn_in['Wd'], 'L0_ffn_bd': _L0_ffn_in['bd'], 'L0_ffn_Wq': _L0_ffn_in['Wq'], 'L0_ffn_keys': _L0_ffn_in['keys'], 'L0_ffn_down_embed': _L0_ffn_in['down_embed'], 'L0_ffn_up_embed': _L0_ffn_in['up_embed']}
    _x0 = _d['L0_attn_x']
    _d['L0_attn_x'] = jax.random.normal(jax.random.fold_in(jax.random.key(seed), 1), (4, 1024, 128), dtype=_x0.dtype)
    del _x0
    return _d

def reference(L0_attn_x, L0_attn_Wqkv, L0_attn_Wproj, L0_ffn_Wg, L0_ffn_bg, L0_ffn_Wu, L0_ffn_bu, L0_ffn_Wd, L0_ffn_bd, L0_ffn_Wq, L0_ffn_keys, L0_ffn_down_embed, L0_ffn_up_embed):

    def _L0_attn_ref(x, Wqkv, Wproj):
        import jax, jax.numpy as jnp
        import numpy as np
        import math
        N_HEAD = 16
        N_EMBD = 128
        HEAD_DIM = N_EMBD // N_HEAD
        ROPE_BASE = 10000.0

        def _rope_cos_sin(T, dh, dtype):
            inv_freq = 1.0 / ROPE_BASE ** (jnp.arange(0, dh, 2, dtype=jnp.float32) / dh)
            freqs = jnp.arange(T, dtype=jnp.float32)[:, None] * inv_freq[None, :]
            cos = jnp.repeat(jnp.cos(freqs), 2, axis=-1).astype(dtype)
            sin = jnp.repeat(jnp.sin(freqs), 2, axis=-1).astype(dtype)
            return (cos, sin)

        def _apply_rope(x, cos, sin):
            x_even = x[..., ::2]
            x_odd = x[..., 1::2]
            x_rot = jnp.stack((-x_odd, x_even), axis=-1).reshape(x.shape)
            return x * cos + x_rot * sin
        B, T, C = x.shape
        H, Dh = (N_HEAD, HEAD_DIM)
        qkv = x @ Wqkv
        q, k, v = jnp.split(qkv, 3, axis=-1)
        Q = q.reshape(B, T, H, Dh).transpose(0, 2, 1, 3)
        K = k.reshape(B, T, H, Dh).transpose(0, 2, 1, 3)
        V = v.reshape(B, T, H, Dh).transpose(0, 2, 1, 3)
        cos, sin = _rope_cos_sin(T, Dh, x.dtype)
        Q = _apply_rope(Q, cos, sin)
        K = _apply_rope(K, cos, sin)
        scores = jnp.einsum('bhqd,bhkd->bhqk', Q, K) / math.sqrt(Dh)
        causal = jnp.tril(jnp.ones((T, T), dtype=bool))
        scores = jnp.where(causal, scores, jnp.finfo(scores.dtype).min)
        attn = jax.nn.softmax(scores, axis=-1)
        y = jnp.einsum('bhqk,bhkd->bhqd', attn, V)
        y = y.transpose(0, 2, 1, 3).reshape(B, T, C)
        return y @ Wproj

    def _L0_ffn_ref(hidden_states, Wg, bg, Wu, bu, Wd, bd, Wq, keys, down_embed, up_embed):
        import jax, jax.numpy as jnp
        import numpy as np
        B, T, D = (2, 256, 128)
        DCD = 512
        RET = 128
        NEXP = 512
        NKEYS = 64
        H = 4
        KPH = 8
        b, t, d = hidden_states.shape
        q = (hidden_states @ Wq).reshape(b, t, 2, H, RET // 2)
        sim = jnp.einsum('btphn,hkpn->pbthk', q, keys)
        sc, ix = jax.lax.top_k(sim, KPH)
        sx, sy = (sc[0], sc[1])
        ixx, ixy = (ix[0], ix[1])
        all_sc = (sx[..., :, None] + sy[..., None, :]).reshape(b, t, H, KPH * KPH)
        all_ix = (ixx[..., :, None] * NKEYS + ixy[..., None, :]).reshape(b, t, H, KPH * KPH)
        scores, pk = jax.lax.top_k(all_sc, KPH)
        idx = jnp.take_along_axis(all_ix, pk, axis=-1)
        de = down_embed[idx]
        ue = up_embed[idx]
        w = jnp.einsum('btd,bthkd->bthk', hidden_states, de)
        w = jax.nn.silu(w) * jax.nn.softmax(scores, axis=-1)
        experts_states = jnp.einsum('bthk,bthkd->btd', w, ue)
        mlp = jax.nn.silu(hidden_states @ Wg + bg) * (hidden_states @ Wu + bu) @ Wd + bd
        return mlp + experts_states
    x = L0_attn_x
    xn = _layernorm(x, axis=-1)
    x = x + _L0_attn_ref(xn, L0_attn_Wqkv, L0_attn_Wproj) + _L0_ffn_ref(xn, L0_ffn_Wg, L0_ffn_bg, L0_ffn_Wu, L0_ffn_bu, L0_ffn_Wd, L0_ffn_bd, L0_ffn_Wq, L0_ffn_keys, L0_ffn_down_embed, L0_ffn_up_embed)
    return x

_drawn_inputs = setup_inputs


def setup_inputs(seed=0):
    import zlib

    import numpy as np

    out = dict(_drawn_inputs(seed))
    spreads = {'L0_ffn_bg': (0.0, 0.8), 'L0_ffn_bu': (0.0, 0.8), 'L0_ffn_bd': (0.0, 0.1)}
    factors = {'L0_ffn_Wg': 4.415,
     'L0_ffn_Wu': 4.352,
     'L0_ffn_Wd': 3.952,
     'L0_ffn_Wq': 8.0,
     'L0_ffn_keys': 8.0,
     'L0_ffn_down_embed': 7.042,
     'L0_ffn_up_embed': 7.631}
    for name, (base, spread) in spreads.items():
        noise = np.random.default_rng([zlib.crc32(name.encode()), seed]).standard_normal(out[name].shape)
        drawn = base * np.exp(spread * noise) if base else spread * noise
        out[name] = jnp.asarray(drawn.astype(out[name].dtype))
    for name, factor in factors.items():
        out[name] = (out[name] * factor).astype(out[name].dtype)
    return out
```

```python
import numpy as np
import concourse.bass as bass
from concourse import mybir
from contextlib import ExitStack

F32 = mybir.dt.float32
BF16 = mybir.dt.bfloat16
ALU = mybir.AluOpType
ACT = mybir.ActivationFunctionType
AX = mybir.AxisListType

START = 1

B, T, D = 4, 1024, 128
H, DH = 16, 8
F = 512
NEXP, NKEYS, RH, KPH = 512, 64, 4, 8
HALF = D // 2
P = 128
NT = T // P
CHUNK = 512
NC = T // CHUNK
TPC = CHUNK // P
NF = F // P
PAIRS = H // 2
GROUPS = H // 4
XI = NEXP // NKEYS
TERMS = [(0, 0), (0, 1), (1, 0), (0, 2), (1, 1), (2, 0)]
KQ = len(TERMS) * DH
KM = KQ + 3
SCALE = float(DH) ** -0.5
MASKED = -1.0e30
EPS = 1e-5
NCAND = 20



def max_units(c):
    units = []
    for i in range(c * TPC, (c + 1) * TPC):
        for k0 in range(0, P * (i + 1), CHUNK):
            w = min(CHUNK, P * (i + 1) - k0)
            n = max(1, CHUNK // w)
            units += [(i, k0, w, list(range(h + e, h + 2 * n, 2))) for h in range(0, H, 2 * n) for e in range(2)]
    return units


def exp_units(c):
    return [(g, kt, u, max(0, kt - c * TPC) * P)
            for g in range(GROUPS) for kt in range((c + 1) * TPC) for u in range(2)]


def build_schedule():
    prep = [("xT", c) for c in range(NC)]
    for n in range(NT + 1):
        if n < NT:
            prep.append(("qkv", n))
        if n >= 1:
            prep.append(("parts", n - 1))
    slots = {}

    def put(phase, step, task):
        slots.setdefault((phase, step), []).append(task)

    def spread(phase, first, last, tasks):
        for k, t in enumerate(tasks):
            put(phase, first + k * (last - first) // len(tasks), t)

    def mlp(c):
        return ([("down", c, f) for f in range(NF)] + [("gate", c, f) for f in range(NF)]
                + [("up", c, f) for f in range(NF)])

    u0, u1, m0 = len(exp_units(0)), len(exp_units(1)), len(max_units(0))
    spread("B", 0, m0, mlp(0))
    for k in range(TPC):
        at = k * u0 // TPC
        put("C", at, ("sim", k))
        put("C", at + 2, ("weights", k))
        put("C", at + 4, ("coefs", k))
    for g in range(GROUPS):
        at = (g + 1) * u0 // GROUPS
        put(*(("C", at) if at < u0 else ("D", 0)), ("ycopy", 0, g))
        put(*(("C", at + 1) if at < u0 else ("D", 1)), ("y", 0, g))
    spread("D", 3, 19, [("yT", 0)] + [("experts", 0, e) for e in range(NF)] + [("out", 0), ("outT", 0)])
    for k in range(TPC):
        at = 2 + k * 13
        put("D", at, ("sim", TPC + k))
        put("D", at + 2, ("weights", TPC + k))
        put("D", at + 4, ("coefs", TPC + k))
    spread("D", 20, 44, mlp(1))
    for g in range(GROUPS - 1):
        at = (g + 1) * u1 // GROUPS
        put("D", at, ("ycopy", 1, g))
        put("D", at + 1, ("y", 1, g))
    tail = [("ycopy", 1, GROUPS - 1), ("y", 1, GROUPS - 1), ("yT", 1)] \
        + [("experts", 1, e) for e in range(NF)] + [("out", 1), ("outT", 1)]
    order = list(prep)
    for phase, steps, after in (("B", m0, [("negmaxT", 0)]), ("C", u0, [("negmaxT", 1)]), ("D", u1, tail)):
        for k in range(steps):
            order += slots.get((phase, k), [])
        order += after
    order = [t for t in order if t[0] not in ("weights", "coefs", "ycopy")]
    return prep, slots, tail, {t: k for k, t in enumerate(order)}


PREP, SLOTS, TAIL, WORK = build_schedule()
NWORK = len(WORK)


def pieces(total, parts, k):
    return range(total * k // parts, total * (k + 1) // parts)


class Steps:

    def __init__(self, engine, sem, per_pass):
        self.engine, self.sem, self.per, self.i, self.n = engine, sem, per_pass, 0, 0

    def begin(self, i):
        self.i, self.n = i, 0

    def mark(self, ins):
        ins.then_inc(self.sem, 1)
        self.n += 1
        return self.n

    def need(self, n):
        self.engine.wait_ge(self.sem, START + self.i * self.per + n)

    def end(self):
        assert self.n == self.per, (self.n, self.per)


def build(nc, x, wqkv, wproj, wg, bg, wu, bu, wd, bd, wq, keys, down, up, rope, out):
    ctx = ExitStack()
    with ctx:
        def sb(name, shape, dt=F32):
            return ctx.enter_context(nc.sbuf_tensor(name, shape, dt))

        def sem(name):
            return ctx.enter_context(nc.semaphore(name))

        parts_dram = nc.dram_tensor("parts_scratch", (2, 3, P, T), BF16, kind="Internal").ap()
        negmax_dram = nc.dram_tensor("negmax_scratch", (2, 3, PAIRS, T), BF16, kind="Internal").ap()

        ident = sb("ident", [P, P])
        identb = sb("identb", [P, P], BF16)
        mask_qk = sb("mask_qk", [P, P], BF16)
        mask_kq = sb("mask_kq", [P, P], BF16)
        rope_sb = sb("rope_sb", [P, 2, NT, DH])
        wqkv_sb = sb("wqkv_sb", [P, 3 * D])
        wproj_sb = sb("wproj_sb", [P, D])
        wg_sb = sb("wg_sb", [P, F])
        wu_sb = sb("wu_sb", [P, F])
        wd_sb = sb("wd_sb", [P, NF, D])
        up_sb = sb("up_sb", [P, NF, D])
        downT = sb("downT", [P, NEXP])
        wsim = sb("wsim", [P, 2, RH, NKEYS])
        bg_sb = sb("bg_sb", [P, NF])
        bu_sb = sb("bu_sb", [P, NF])
        bd_sb = sb("bd_sb", [P, 1])
        half_neg = sb("half_neg", [P, NT])
        eps = sb("eps", [P, NT])
        carrier = sb("carrier", [P, 1])
        wq_sb = sb("wq_sb", [P, RH, 2, HALF])
        keys_sb = sb("keys_sb", [NKEYS, RH, 2, HALF])
        down_sb = sb("down_sb", [P, NF, D])
        wqT = sb("wqT", [P, P])
        keysT = sb("keysT", [P, NKEYS])

        xin = sb("xin", [P, NT, D])
        stats = sb("stats", [P, NT, 6])
        meanvar = sb("meanvar", [P, NT, 2])
        vareps = sb("vareps", [P, NT])
        rstd = sb("rstd", [P, NT])
        xn = sb("xn", [P, NT, D])
        xnT = sb("xnT", [P, T])
        qk = sb("qk", [P, 2, 2 * H, DH])
        rot_a = sb("rot_a", [P, 2 * H, DH])
        rot_b = sb("rot_b", [P, 2 * H, DH])
        rot = sb("rot", [P, 2, 2 * H, DH])
        rest = sb("rest", [P, 2 * D])
        parts = sb("parts", [P, 2, 3, 2 * D], BF16)
        partsT = sb("partsT", [P, 2, 3, T], BF16)
        qs = sb("qs", [P, PAIRS, T], BF16)
        ks = sb("ks", [P, PAIRS, T], BF16)
        vaug = sb("vaug", [P, NT, H, 32])

        pmax = sb("pmax", [P, NT, 2, H])
        rmax = sb("rmax", [P, TPC, H])
        mrest = sb("mrest", [P, TPC, H])
        negmax_pad = sb("negmax_pad", [P, TPC, P], BF16)
        negmax = negmax_pad[:, :, 0:3 * H].rearrange("p n (e s j) -> p n e s j", e=2, s=3)
        negmaxT = sb("negmaxT", [3 * H, CHUNK], BF16)
        NPT = 3
        pT = sb("pT", [P, NPT, 2, CHUNK])
        yT4 = sb("yT4", [P, CHUNK])
        ytm = sb("ytm", [P, TPC, H, DH])
        yinv = sb("yinv", [P, TPC, 4])
        yT = sb("yT", [P, CHUNK])

        sgate = sb("sgate", [P, NF, CHUNK])
        hT = sb("hT", [P, NF, CHUNK])
        sexp = sb("sexp", [P, NF, CHUNK])
        gT = sexp
        sim = sb("sim", [P, 2 * RH, NKEYS])
        simx = sb("simx", [P, RH, XI])
        top = sb("top", [P, 2 * RH, KPH])
        cand = sb("cand", [P, RH, NCAND])
        best = sb("best", [P, RH, KPH])
        ND = RH * (KPH + XI + NKEYS)
        dif = sb("dif", [P, ND])
        edif = sb("edif", [P, ND])
        zsum = sb("zsum", [P, RH])
        zinv = sb("zinv", [P, RH])
        exz = sb("exz", [P, RH, XI])
        ssum = sb("ssum", [P, RH, XI, NKEYS])
        wsum = sb("wsum", [P, RH, XI * NKEYS])
        coef4 = sb("coef4", [P, RH, XI * NKEYS])
        csum2 = sb("csum2", [P, 2, XI * NKEYS])
        inside = sb("inside", [P, RH])
        inside1 = sb("inside1", [P, 1])
        clipped = sb("clipped", [P, 1])
        coef = sb("coef", [P, TPC, NEXP])
        oT = sb("oT", [P, CHUNK])
        xres = sb("xres", [P, TPC, D])
        osb = sb("osb", [P, TPC, D])

        work = ctx.enter_context(nc.psum_tensor("work", [P, CHUNK], F32))
        mbank = ctx.enter_context(nc.psum_tensor("mbank", [P, 2, CHUNK], F32))
        sbank = ctx.enter_context(nc.psum_tensor("sbank", [P, 2, 2, CHUNK], F32))
        ybank = ctx.enter_context(nc.psum_tensor("ybank", [P, CHUNK], F32))
        workb = work[:, :].bitcast(BF16)

        weights_loaded = sem("weights_loaded")
        consts_made = sem("consts_made")
        pool_setup = sem("pool_setup")
        setup_filled = sem("setup_filled")
        setup_copied = sem("setup_copied")
        x_loaded = sem("x_loaded")
        res_loaded = sem("res_loaded")
        stats_done = sem("stats_done")
        var_ready = sem("var_ready")
        rstd_ready = sem("rstd_ready")
        xn_ready = sem("xn_ready")
        work_filled = sem("work_filled")
        work_copied = sem("work_copied")
        qk_copied = sem("qk_copied")
        rot_ready = sem("rot_ready")
        parts_ready = sem("parts_ready")
        parts_stored = sem("parts_stored")
        parts_loaded = sem("parts_loaded")
        max_filled = sem("max_filled")
        max_read = sem("max_read")
        negmax_ready = sem("negmax_ready")
        negmax_stored = sem("negmax_stored")
        negmax_loaded = sem("negmax_loaded")
        scores_filled = sem("scores_filled")
        probs_ready = sem("probs_ready")
        probs_used = sem("probs_used")
        yT4_ready = sem("yT4_ready")
        dif_ready = sem("dif_ready")
        edif_ready = sem("edif_ready")
        zinv_ready = sem("zinv_ready")
        pairs_ready = sem("pairs_ready")
        weighed = sem("weighed")
        clipped_ready = sem("clipped_ready")
        kept_ready = sem("kept_ready")
        coef_ready = sem("coef_ready")
        out_stored = sem("out_stored")
        pool_steps = sem("pool_steps")
        dve_steps = sem("dve_steps")

        block = ctx.enter_context(nc.Block())
        x_v = x.rearrange("b (n p) d -> b p n d", p=P)
        o_v = out.rearrange("b (n p) d -> b p n d", p=P)
        NLOAD = 15
        NCONST = 9
        NSTACK = len(TERMS) * 2 * 2

        NU = [len(exp_units(c)) for c in range(NC)]
        NM = [len(max_units(c)) for c in range(NC)]
        UNITS, MUNITS = sum(NU), sum(NM)
        SETUP = [downT[:, t * P:(t + 1) * P] for t in range(NF)]
        for h in range(RH):
            SETUP += [wqT[:, :], keysT[:, :], wsim[:, 0, h, :], wsim[:, 1, h, :]]

        def filled(e, i, task):
            e.wait_ge(work_filled, START + i * NWORK + WORK[task] + 1)

        def copied(e, i, task):
            e.wait_ge(work_copied, START + i * NWORK + WORK[task] + 1)

        def filled_before(e, i, task=None):
            e.wait_ge(work_filled, START + i * NWORK + (WORK[task] + 1 if task else 0))

        @block.sync
        def _(sp):
            for dst, src in [
                (wqkv_sb[:, :], wqkv), (wproj_sb[:, :], wproj), (wg_sb[:, :], wg), (wu_sb[:, :], wu),
                (wd_sb[:, :, :], wd.rearrange("(t p) c -> p t c", p=P)),
                (up_sb[:, :, :], up.rearrange("(t p) c -> p t c", p=P)),
                (down_sb[:, :, :], down.rearrange("(t p) c -> p t c", p=P)),
                (wq_sb[:, :, 0, :], wq[:, 0:RH * HALF].rearrange("d (h n) -> d h n", h=RH)),
                (wq_sb[:, :, 1, :], wq[:, RH * HALF:].rearrange("d (h n) -> d h n", h=RH)),
                (keys_sb[:, :, :, :], keys.rearrange("h k a n -> k h a n")),
                (bg_sb[:, :], bg.rearrange("(t p) -> p t", p=P)),
                (bu_sb[:, :], bu.rearrange("(t p) -> p t", p=P)),
                (bd_sb[:, :], bd.rearrange("(p a) -> p a", a=1)),
                (rope_sb[:, 0, :, :], rope[0].rearrange("(n p) d -> p n d", p=P)),
                (rope_sb[:, 1, :, :], rope[1].rearrange("(n p) d -> p n d", p=P)),
            ]:
                sp.dma_start(dst, src, allow_slow_non_contiguous=True).then_inc(weights_loaded, 16)

            for s in (x_loaded, res_loaded, parts_stored, parts_loaded, negmax_stored, negmax_loaded, out_stored):
                sp.sem_inc(s, START)
            with sp.Fori(0, B) as i:
                def load_rows(dst, n0, n1, loaded):
                    sp.dma_start(dst, x_v[bass.ds(i, 1), :, n0:n1, :].rearrange("b p n d -> (b p) n d"))\
                        .then_inc(loaded, 16)

                sp.wait_ge(xn_ready, START + i * NT)
                load_rows(xin[:, :, :], 0, NT, x_loaded)
                sp.wait_ge(work_copied, START + i * NWORK)
                load_rows(xres[:, :, :], 0, TPC, res_loaded)
                copied(sp, i, ("parts", NT - 1))
                for s in range(3):
                    for a in range(2):
                        sp.dma_start(parts_dram[a, s], partsT[:, a, s, :]).then_inc(parts_stored, 16)
                sp.wait_ge(parts_stored, START + (i + 1) * (6 * 16))
                for t, pair in enumerate(TERMS):
                    for a, dst in ((0, qs), (1, ks)):
                        for hh in range(2):
                            src = parts_dram[a, pair[a]].rearrange("(j h d) t -> h d j t", h=2, d=DH)[hh]
                            r = HALF * hh + DH * t
                            sp.dma_start(dst[r:r + DH, :, :], src).then_inc(parts_loaded, 16)
                for c in range(NC):
                    cols = slice(c * CHUNK, (c + 1) * CHUNK)
                    copied(sp, i, ("negmaxT", c))
                    sp.dma_start(negmax_dram.rearrange("h s j t -> (h s j) t")[:, cols], negmaxT[:, :])\
                        .then_inc(negmax_stored, 16)
                    sp.wait_ge(negmax_stored, START + (i * NC + c + 1) * 16)
                    for hh in range(2):
                        r = HALF * hh + KQ
                        sp.dma_start(qs[r:r + 3, :, cols], negmax_dram[hh][:, :, cols]).then_inc(negmax_loaded, 16)
                for c in range(NC):
                    copied(sp, i, ("outT", c))
                    sp.dma_start(o_v[bass.ds(i, 1), :, c * TPC:(c + 1) * TPC, :].rearrange("b p n d -> (b p) n d"),
                                 osb[:, :, :]).then_inc(out_stored, 16)
                    if c == 0:
                        load_rows(xres[:, :, :], TPC, NT, res_loaded)
            sp.wait_ge(out_stored, START + B * NC * 16)

        @block.gpsimd
        def _(pool):
            g = nc.gpsimd
            for m in (ident, identb, mask_qk, mask_kq):
                g.memset(m[:, :], 0.0).then_inc(pool_setup, 1)
            pool.wait_ge(pool_setup, 4)
            for m in (ident, identb):
                g.affine_select(out=m[:, :], in_=m[:, :], pattern=[[-1, P]], compare_op=ALU.not_equal, fill=1.0,
                                base=0, channel_multiplier=1).then_inc(consts_made, 1)
            g.affine_select(out=mask_qk[:, :], in_=mask_qk[:, :], pattern=[[-1, P]], compare_op=ALU.is_ge,
                            fill=MASKED, base=0, channel_multiplier=1).then_inc(consts_made, 1)
            g.affine_select(out=mask_kq[:, :], in_=mask_kq[:, :], pattern=[[1, P]], compare_op=ALU.is_ge,
                            fill=MASKED, base=0, channel_multiplier=-1).then_inc(consts_made, 1)
            g.memset(half_neg[:, :], -0.5).then_inc(consts_made, 1)
            g.memset(eps[:, :], EPS).then_inc(consts_made, 1)
            g.memset(negmax_pad[:, :, :], 0.0).then_inc(consts_made, 1)
            g.memset(ks[:, :, :], 1.0).then_inc(consts_made, 1)
            g.memset(vaug[:, :, :, :], 0.0).then_inc(pool_setup, 1)
            pool.wait_ge(pool_setup, 5)
            g.memset(vaug[:, :, :, DH:DH + 1], 1.0).then_inc(consts_made, 1)
            pool.wait_ge(weights_loaded, 16 * NLOAD)
            pool.wait_ge(consts_made, NCONST)
            steps = Steps(pool, pool_steps, 6 * NT)
            for s in (var_ready, rstd_ready, rot_ready, pairs_ready, weighed, coef_ready, pool_steps):
                pool.sem_inc(s, START)
            with pool.Fori(0, B) as i:
                steps.begin(i)
                pool.wait_ge(stats_done, START + (i + 1) * NT)
                pool.wait_ge(xn_ready, START + i * NT)
                g.tensor_tensor(vareps[:, :], meanvar[:, :, 1], eps[:, :], ALU.add).then_inc(var_ready, 1)
                pool.wait_ge(var_ready, START + i + 1)
                g.tensor_tensor(rstd[:, :], vareps[:, :], half_neg[:, :], ALU.pow).then_inc(rstd_ready, 1)
                for n in range(NT):
                    pool.wait_ge(qk_copied, START + i * NT + n + 1)
                    a = qk[:, n % 2, :, :]
                    cos = rope_sb[:, 0, n:n + 1, :].to_broadcast([P, 2 * H, DH])
                    sin = rope_sb[:, 1, n:n + 1, :].rearrange("p o (e t) -> p o e t", t=2)
                    a2 = a.rearrange("p h (e t) -> p h e t", t=2)
                    b2 = rot_b[:, :, :].rearrange("p h (e t) -> p h e t", t=2)
                    steps.mark(g.tensor_tensor(rot_a[:, :, :], a, cos, ALU.mult))
                    for t in range(2):
                        k = steps.mark(g.tensor_tensor(b2[:, :, :, t], a2[:, :, :, 1 - t],
                                                       sin[:, :, :, t].to_broadcast([P, 2 * H, DH // 2]), ALU.mult))
                    steps.need(k)
                    pool.wait_ge(parts_ready, START + i * NT + max(n - 1, 0))
                    g.tensor_tensor(rot[:, n % 2, :, :], rot_a[:, :, :], rot_b[:, :, :], ALU.add)\
                        .then_inc(rot_ready, 1)
                    pool.wait_ge(rot_ready, START + i * NT + n + 1)
                for n in range(NT):
                    copied(pool, i, ("sim", n))
                    pool.wait_ge(kept_ready, START + (i * NT + n) * RH)
                    for h in range(RH):
                        g.tensor_tensor(ssum[:, h, :, :],
                                        sim[:, h, 0:XI].unsqueeze(2).to_broadcast([P, XI, NKEYS]),
                                        sim[:, RH + h:RH + h + 1, :].to_broadcast([P, XI, NKEYS]), ALU.add)\
                            .then_inc(pairs_ready, 1)
                    pool.wait_ge(zinv_ready, START + i * NT + n + 1)
                    k = steps.mark(g.tensor_tensor(
                        exz[:, :, :], edif[:, RH * KPH:RH * (KPH + XI)].rearrange("p (h i) -> p h i", h=RH),
                        zinv[:, :].unsqueeze(2).to_broadcast([P, RH, XI]), ALU.mult))
                    steps.need(k)
                    ey = edif[:, RH * (KPH + XI):].rearrange("p (h j) -> p h j", h=RH)
                    for h in range(RH):
                        g.tensor_tensor(wsum[:, h, :].rearrange("p (i j) -> p i j", i=XI),
                                        exz[:, h, :].unsqueeze(2).to_broadcast([P, XI, NKEYS]),
                                        ey[:, h:h + 1, :].to_broadcast([P, XI, NKEYS]), ALU.mult)\
                            .then_inc(weighed, 1)
                    pool.wait_ge(kept_ready, START + (i * NT + n + 1) * RH)
                    k = steps.mark(g.tensor_tensor(csum2[:, :, :], coef4[:, 0:2, :], coef4[:, 2:4, :], ALU.add))
                    steps.need(k)
                    filled_before(pool, i, ("experts", n // TPC - 1, NF - 1) if n >= TPC else None)
                    c = n % TPC
                    pool.wait_ge(clipped_ready, START + i * NT + n + 1)
                    k = steps.mark(g.tensor_tensor(coef[:, c, :], csum2[:, 0, :], csum2[:, 1, :], ALU.add))
                    steps.need(k)
                    g.tensor_tensor(coef[:, c, NEXP - 1:NEXP], coef[:, c, NEXP - 1:NEXP], clipped[:, :], ALU.add)\
                        .then_inc(coef_ready, 1)
                    pool.wait_ge(coef_ready, START + i * NT + n + 1)
                steps.end()

        @block.scalar
        def _(act):
            a = nc.scalar
            for n, dst in enumerate(SETUP):
                act.wait_ge(setup_filled, n + 1)
                a.activation(dst, work[:, 0:dst.shape[-1]], ACT.Copy).then_inc(setup_copied, 1)
            act.wait_ge(weights_loaded, 16 * NLOAD)
            act.wait_ge(consts_made, NCONST)
            for s in (qk_copied, yT4_ready, edif_ready, probs_ready, work_copied):
                act.sem_inc(s, START)
            with act.Fori(0, B) as i:
                def task(t):
                    kind = t[0]
                    if kind in ("xT", "qkv", "parts", "negmaxT", "down", "gate", "sim", "yT", "out"):
                        filled(act, i, t)
                    if kind == "xT":
                        c = t[1]
                        a.activation(xnT[:, c * CHUNK:(c + 1) * CHUNK], work[:, :], ACT.Copy)\
                            .then_inc(work_copied, 1)
                    elif kind == "qkv":
                        n = t[1]
                        act.wait_ge(rot_ready, START + i * NT + max(n - 1, 0))
                        a.activation(qk[:, n % 2, :, :], work[:, 0:2 * D].rearrange("p (h d) -> p h d", d=DH),
                                     ACT.Copy).then_inc(qk_copied, 1)
                        act.wait_ge(probs_used, START + i * UNITS)
                        a.activation(vaug[:, n, :, 0:DH],
                                     work[:, 2 * D:3 * D].rearrange("p (h d) -> p h d", d=DH),
                                     ACT.Copy).then_inc(work_copied, 1)
                    elif kind == "parts":
                        n = t[1]
                        act.wait_ge(parts_stored, START + i * 6 * 16)
                        a.activation(partsT[:, :, :, n * P:(n + 1) * P].rearrange("p a s t -> p (a s) t"),
                                     workb[:, 0:6 * P].rearrange("p (a t) -> p a t", t=P), ACT.Copy)\
                            .then_inc(work_copied, 1)
                    elif kind == "negmaxT":
                        act.wait_ge(negmax_stored, START + (i * NC + t[1]) * 16)
                        a.activation(negmaxT[:, :], workb[0:3 * H, 0:CHUNK], ACT.Copy).then_inc(work_copied, 1)
                    elif kind == "down":
                        a.activation(sexp[:, t[2], :], work[:, :], ACT.Silu).then_inc(work_copied, 1)
                    elif kind == "gate":
                        a.activation(sgate[:, t[2], :], work[:, :], ACT.Silu, bias=bg_sb[:, t[2]:t[2] + 1])\
                            .then_inc(work_copied, 1)
                    elif kind == "sim":
                        n = t[1]
                        act.wait_ge(dif_ready, START + i * NT + n)
                        act.wait_ge(pairs_ready, START + (i * NT + n) * RH)
                        a.activation(sim[:, :, :], work[:, :].rearrange("p (g k) -> p g k", k=NKEYS), ACT.Copy)\
                            .then_inc(work_copied, 1)
                    elif kind == "weights":
                        n = t[1]
                        act.wait_ge(dif_ready, START + i * NT + n + 1)
                        act.wait_ge(weighed, START + (i * NT + n) * RH)
                        a.activation(edif[:, :], dif[:, :], ACT.Exp).then_inc(edif_ready, 1)
                    elif kind == "ycopy":
                        k = t[1] * GROUPS + t[2]
                        act.wait_ge(probs_used, START + i * UNITS + sum(NU[:t[1]]) + (t[2] + 1) * NU[t[1]] // GROUPS)
                        filled_before(act, i, ("y", (k - 1) // GROUPS, (k - 1) % GROUPS) if k else None)
                        a.activation(yT4[:, :], ybank[:, :], ACT.Copy).then_inc(yT4_ready, 1)
                    elif kind == "yT":
                        a.activation(yT[:, :], work[:, :], ACT.Copy).then_inc(work_copied, 1)
                    elif kind == "out":
                        a.activation(oT[:, :], work[:, :], ACT.Identity, bias=bd_sb[:, 0:1])\
                            .then_inc(work_copied, 1)

                def side(phase, step):
                    for t in SLOTS.get((phase, step), []):
                        task(t)

                for t in PREP:
                    task(t)
                for m in range(NM[0]):
                    side("B", m)
                task(("negmaxT", 0))
                for c in range(NC):
                    for n, (gr, kt, u, q0) in enumerate(exp_units(c)):
                        k = sum(NU[:c]) + n
                        act.wait_ge(scores_filled, START + i * UNITS + k + 1)
                        act.wait_ge(probs_used, START + i * UNITS + max(k + 1 - NPT, 0))
                        a.activation(pT[:, k % NPT, :, q0:CHUNK], sbank[:, k % 2, :, q0:CHUNK], ACT.Exp,
                                     scale=SCALE).then_inc(probs_ready, 1)
                        side("CD"[c], n)
                    if c == 0:
                        task(("negmaxT", 1))
                for t in TAIL:
                    task(t)

        @block.vector
        def _(dve):
            v = nc.vector
            TOP_STEPS = 1 + 2 * RH + 4 + 2 + RH + 2
            steps = Steps(dve, dve_steps, NT + 3 * NT + (1 + 3) + (2 + 3) + NT * TOP_STEPS + NC * GROUPS)
            dve.wait_ge(weights_loaded, 16 * NLOAD)
            for s in (stats_done, xn_ready, parts_ready, max_read, negmax_ready, dif_ready, zinv_ready, kept_ready,
                      clipped_ready, dve_steps):
                dve.sem_inc(s, START)
            with dve.Fori(0, B) as i:
                steps.begin(i)

                def best_pairs(n):
                    copied(dve, i, ("sim", n))
                    dve.wait_ge(kept_ready, START + (i * NT + n) * RH)
                    steps.mark(v.tensor_copy(simx[:, :, :], sim[:, 0:RH, 0:XI]))
                    for a in range(2 * RH):
                        k = steps.mark(v.max(top[:, a, :], sim[:, a, :]))
                    steps.need(k)
                    xs, ys = top[:, 0:RH, :], top[:, RH:2 * RH, :]

                    def wide(ap, w):
                        return ap.to_broadcast([P, RH, w])

                    steps.mark(v.tensor_tensor(cand[:, :, 0:8], ys, wide(xs[:, :, 0:1], 8), ALU.add))
                    steps.mark(v.tensor_tensor(cand[:, :, 8:12], ys[:, :, 0:4], wide(xs[:, :, 1:2], 4), ALU.add))
                    steps.mark(v.tensor_tensor(cand[:, :, 12:16].rearrange("p h (a b) -> p h a b", a=2),
                                               ys[:, :, 0:2].unsqueeze(2).to_broadcast([P, RH, 2, 2]),
                                               xs[:, :, 2:4].unsqueeze(3).to_broadcast([P, RH, 2, 2]), ALU.add))
                    k = steps.mark(v.tensor_tensor(cand[:, :, 16:20], xs[:, :, 4:8], wide(ys[:, :, 0:1], 4),
                                                   ALU.add))
                    dve.wait_ge(edif_ready, START + i * NT + n)
                    steps.need(k)
                    o = RH * KPH
                    steps.mark(v.tensor_tensor(dif[:, o:o + RH * XI].rearrange("p (h i) -> p h i", h=RH),
                                               simx[:, :, :], wide(xs[:, :, 0:1], XI), ALU.subtract))
                    o += RH * XI
                    steps.mark(v.tensor_tensor(dif[:, o:].rearrange("p (h j) -> p h j", h=RH),
                                               sim[:, RH:2 * RH, :], wide(ys[:, :, 0:1], NKEYS), ALU.subtract))
                    for h in range(RH):
                        k = steps.mark(v.max(best[:, h, :], cand[:, h, :]))
                    steps.need(k)
                    v.tensor_tensor(dif[:, 0:RH * KPH].rearrange("p (h r) -> p h r", h=RH), best[:, :, :],
                                    wide(best[:, :, 0:1], KPH), ALU.subtract).then_inc(dif_ready, 1)

                def keep_best(n):
                    dve.wait_ge(edif_ready, START + i * NT + n + 1)
                    k = steps.mark(v.tensor_reduce(zsum[:, :],
                                                   edif[:, 0:RH * KPH].rearrange("p (h r) -> p h r", h=RH),
                                                   axis=AX.X, op=ALU.add))
                    steps.need(k)
                    dve.wait_ge(weighed, START + (i * NT + n) * RH)
                    v.reciprocal(zinv[:, :], zsum[:, :]).then_inc(zinv_ready, 1)
                    dve.wait_ge(coef_ready, START + i * NT + n)
                    for h in range(RH):
                        dve.wait_ge(weighed, START + (i * NT + n) * RH + h + 1)
                        v.scalar_tensor_tensor(out=coef4[:, h, :], in0=ssum[:, h, :, :].rearrange("p i j -> p (i j)"),
                                               scalar=best[:, h, KPH - 1:KPH], in1=wsum[:, h, :],
                                               op0=ALU.is_ge, op1=ALU.mult, accum_out=inside[:, h:h + 1])\
                            .then_inc(kept_ready, 1)
                    dve.wait_ge(kept_ready, START + (i * NT + n + 1) * RH)
                    k = steps.mark(v.tensor_reduce(inside1[:, :], inside[:, :], axis=AX.X, op=ALU.add))
                    steps.need(k)
                    v.tensor_scalar(clipped[:, :], inside1[:, :], -1.0, float(RH), ALU.mult, ALU.add)\
                        .then_inc(clipped_ready, 1)

                def task(t):
                    kind = t[0]
                    if kind in ("up", "experts", "y", "outT"):
                        filled(dve, i, t)
                    if kind == "up":
                        f = t[2]
                        v.scalar_tensor_tensor(out=hT[:, f, :], in0=work[:, :], scalar=bu_sb[:, f:f + 1],
                                               in1=sgate[:, f, :], op0=ALU.add, op1=ALU.mult)\
                            .then_inc(work_copied, 1)
                    elif kind == "experts":
                        e = t[2]
                        v.tensor_tensor(gT[:, e, :], work[:, :], sexp[:, e, :], ALU.mult).then_inc(work_copied, 1)
                    elif kind == "y":
                        _, c, gr = t
                        wv = work[:, :].rearrange("p (n j d) -> p n j d", n=TPC, j=4)
                        s = steps.mark(v.reciprocal(yinv[:, :, :], wv[:, :, :, DH]))
                        steps.need(s)
                        v.tensor_tensor(ytm[:, :, 4 * gr:4 * gr + 4, :], wv[:, :, :, 0:DH],
                                        yinv[:, :, :].unsqueeze(3).to_broadcast([P, TPC, 4, DH]), ALU.mult)\
                            .then_inc(work_copied, 1)
                    elif kind == "outT":
                        c = t[1]
                        dve.wait_ge(res_loaded, START + 16 * (i * NC + c + 1))
                        dve.wait_ge(out_stored, START + 16 * (i * NC + c))
                        v.tensor_tensor(osb[:, :, :], work[:, :].rearrange("p (n d) -> p n d", d=D), xres[:, :, :],
                                        ALU.add).then_inc(work_copied, 1)
                    elif kind == "sim":
                        best_pairs(t[1])
                    elif kind == "coefs":
                        keep_best(t[1])

                def side(phase, step):
                    for t in SLOTS.get((phase, step), []):
                        task(t)

                def max_unit(k, unit):
                    it, k0, w, heads = unit
                    dve.wait_ge(max_filled, START + i * MUNITS + k + 1)
                    v.tensor_reduce(pmax[:, it, k0 // CHUNK, heads[0]:heads[-1] + 1:2],
                                    mbank[:, k % 2, 0:w * len(heads)].rearrange("p (h w) -> p h w", w=w),
                                    axis=AX.X, op=ALU.max).then_inc(max_read, 1)

                def negated(c):
                    dve.wait_ge(max_read, START + i * MUNITS + sum(NM[:c + 1]))
                    n = slice(c * TPC, (c + 1) * TPC)
                    m = pmax[:, n, 0, :]
                    if c > 0:
                        k = steps.mark(v.tensor_tensor(mrest[:, :, :], m, pmax[:, n, 1, :], ALU.max))
                        steps.need(k)
                        m = mrest[:, :, :]
                    k = steps.mark(v.tensor_scalar(rmax[:, :, :], m, -1.0, None, ALU.mult))
                    steps.need(k)
                    filled_before(dve, i, ("negmaxT", c - 1) if c else None)
                    pj = [ap.rearrange("p n (j e) -> p n e j", e=2) for ap in (rmax[:, :, :], mrest[:, :, :])]
                    k = steps.mark(v.tensor_copy(negmax[:, :, :, 0, :], pj[0]))
                    steps.need(k)
                    k = steps.mark(v.tensor_tensor(pj[1], pj[0], negmax[:, :, :, 0, :], ALU.subtract))
                    steps.need(k)
                    k = steps.mark(v.tensor_copy(negmax[:, :, :, 1, :], pj[1]))
                    steps.need(k)
                    v.tensor_tensor(negmax[:, :, :, 2, :], pj[1], negmax[:, :, :, 1, :], ALU.subtract)\
                        .then_inc(negmax_ready, 1)

                dve.wait_ge(x_loaded, START + 16 * (i + 1))
                for n in range(NT):
                    k = steps.mark(v.bn_stats(stats[:, n, :], xin[:, n, :]))
                steps.need(k)
                v.memset(carrier[:, :], 0.0)
                for n in range(NT):
                    v.bn_aggr(meanvar[:, n, :], stats[:, n, :]).then_inc(stats_done, 1)
                dve.wait_ge(stats_done, START + (i + 1) * NT)
                dve.wait_ge(rstd_ready, START + i + 1)
                filled_before(dve, i)
                for n in range(NT):
                    v.tensor_scalar(xn[:, n, :], xin[:, n, :], meanvar[:, n, 0:1], rstd[:, n:n + 1],
                                    ALU.subtract, ALU.mult).then_inc(xn_ready, 1)
                for n in range(NT):
                    dve.wait_ge(rot_ready, START + i * NT + n + 1)
                    filled_before(dve, i, ("parts", n - 2) if n >= 2 else None)
                    r = rot[:, n % 2, :, :].rearrange("p h d -> p (h d)")
                    pt = parts[:, n % 2, :, :]
                    k = steps.mark(v.tensor_copy(pt[:, 0, :], r))
                    steps.need(k)
                    k = steps.mark(v.tensor_tensor(rest[:, :], r, pt[:, 0, :], ALU.subtract))
                    steps.need(k)
                    k = steps.mark(v.tensor_copy(pt[:, 1, :], rest[:, :]))
                    steps.need(k)
                    v.tensor_tensor(pt[:, 2, :], rest[:, :], pt[:, 1, :], ALU.subtract).then_inc(parts_ready, 1)
                    dve.wait_ge(parts_ready, START + i * NT + n + 1)
                for k, unit in enumerate(max_units(0)):
                    max_unit(k, unit)
                    side("B", k)
                negated(0)
                later = max_units(1)
                for n in range(NU[0]):
                    for m in pieces(NM[1], NU[0], n):
                        max_unit(NM[0] + m, later[m])
                    side("C", n)
                negated(1)
                for n in range(NU[1]):
                    side("D", n)
                for t in TAIL:
                    task(t)
                steps.end()

        @block.tensor
        def _(pe):
            t_ = nc.tensor
            pe.wait_ge(weights_loaded, 16 * NLOAD)
            pe.wait_ge(consts_made, NCONST)
            n = 0

            def setup_done(ins):
                nonlocal n
                ins.then_inc(setup_filled, 1)
                n += 1
                pe.wait_ge(setup_copied, n)

            for t in range(NF):
                setup_done(t_.transpose(work[:, 0:P], down_sb[:, t, :], ident[:, :]))
            for h in range(RH):
                setup_done(t_.transpose(work[:, 0:P], wq_sb[:, h, :, :].rearrange("p a n -> p (a n)"), ident[:, :]))
                setup_done(t_.transpose(work[:, 0:NKEYS], keys_sb[:, h, :, :].rearrange("k a n -> k (a n)"), ident[0:NKEYS, 0:NKEYS]))
                for s in range(2):
                    r = slice(HALF * s, HALF * (s + 1))
                    setup_done(t_.matmul(work[:, 0:NKEYS], wqT[r, :], keysT[r, :], start=True, stop=True))

            for s in (work_filled, max_filled, scores_filled, probs_used):
                pe.sem_inc(s, START)
            with pe.Fori(0, B) as i:
                def tokens(c):
                    return slice(c * CHUNK, (c + 1) * CHUNK)

                def task(t):
                    kind = t[0]
                    if t not in WORK:
                        return
                    pe.wait_ge(work_copied, START + i * NWORK + WORK[t])
                    if kind == "xT":
                        c = t[1]
                        for n in range(TPC):
                            pe.wait_ge(xn_ready, START + i * NT + c * TPC + n + 1)
                            ins = t_.transpose(work[:, n * P:(n + 1) * P], xn[:, c * TPC + n, :], ident[:, :])
                    elif kind == "qkv":
                        n = t[1]
                        ins = t_.matmul(work[:, 0:3 * D], xnT[:, n * P:(n + 1) * P], wqkv_sb[:, :],
                                        start=True, stop=True)
                    elif kind == "parts":
                        n = t[1]
                        pe.wait_ge(parts_ready, START + i * NT + n + 1)
                        for a in range(2):
                            for s in range(3):
                                k = 3 * a + s
                                ins = t_.transpose(workb[:, k * P:(k + 1) * P],
                                                   parts[:, n % 2, s, a * D:(a + 1) * D], identb[:, :])
                    elif kind == "negmaxT":
                        pe.wait_ge(negmax_ready, START + i * NC + t[1] + 1)
                        for n in range(TPC):
                            ins = t_.transpose(workb[:, n * P:(n + 1) * P], negmax_pad[:, n, :], identb[:, :])
                    elif kind in ("down", "gate", "up"):
                        w = {"down": downT, "gate": wg_sb, "up": wu_sb}[kind]
                        ins = t_.matmul(work[:, :], w[:, t[2] * P:(t[2] + 1) * P], xnT[:, tokens(t[1])],
                                        start=True, stop=True)
                    elif kind == "sim":
                        n = t[1]
                        ins = t_.matmul(work[:, :], xnT[:, n * P:(n + 1) * P],
                                        wsim[:, :, :, :].rearrange("p a h k -> p (a h k)"), start=True, stop=True)
                    elif kind == "y":
                        k = t[1] * GROUPS + t[2]
                        pe.wait_ge(yT4_ready, START + i * NC * GROUPS + k + 1)
                        for n in range(TPC):
                            ins = t_.transpose(work[:, n * P:(n + 1) * P], yT4[:, n * P:(n + 1) * P], ident[:, :])
                    elif kind == "yT":
                        for n in range(TPC):
                            ins = t_.transpose(work[:, n * P:(n + 1) * P],
                                               ytm[:, n, :, :].rearrange("p h d -> p (h d)"), ident[:, :])
                    elif kind == "experts":
                        pe.wait_ge(coef_ready, START + i * NT + (t[1] + 1) * TPC)
                        for n in range(TPC):
                            ins = t_.transpose(work[:, n * P:(n + 1) * P], coef[:, n, t[2] * P:(t[2] + 1) * P],
                                               ident[:, :])
                    elif kind == "out":
                        c = t[1]
                        t_.matmul(work[:, :], wproj_sb[:, :], yT[:, :], start=True, stop=False)
                        for f in range(NF):
                            t_.matmul(work[:, :], wd_sb[:, f, :], hT[:, f, :], start=False, stop=False)
                            ins = t_.matmul(work[:, :], up_sb[:, f, :], gT[:, f, :], start=False, stop=f == NF - 1)
                    elif kind == "outT":
                        for n in range(TPC):
                            ins = t_.transpose(work[:, n * P:(n + 1) * P], oT[:, n * P:(n + 1) * P], ident[:, :])
                    ins.then_inc(work_filled, 1)

                def side(phase, step):
                    for t in SLOTS.get((phase, step), []):
                        task(t)

                def max_unit(k, unit):
                    it, k0, w, heads = unit
                    pe.wait_ge(max_read, START + i * MUNITS + max(k - 1, 0))
                    for s, h in enumerate(heads):
                        r = slice(HALF * (h % 2), HALF * (h % 2) + KQ)
                        diag = k0 + w == P * (it + 1)
                        ins = t_.matmul(mbank[:, k % 2, s * w:(s + 1) * w], qs[r, h // 2, it * P:(it + 1) * P],
                                        ks[r, h // 2, k0:k0 + w], start=True, stop=not diag)
                        if diag:
                            ins = t_.matmul(mbank[:, k % 2, (s + 1) * w - P:(s + 1) * w], identb[:, :],
                                            mask_qk[:, :], start=False, stop=True)
                    ins.then_inc(max_filled, 1)

                def scores(c, k, unit):
                    gr, kt, u, q0 = unit
                    pe.wait_ge(probs_ready, START + i * UNITS + max(k - 1, 0))
                    for j in range(2):
                        r = slice(HALF * j, HALF * j + KM)
                        diag = kt >= c * TPC
                        ins = t_.matmul(sbank[:, k % 2, j, q0:CHUNK], ks[r, 2 * gr + u, kt * P:(kt + 1) * P],
                                        qs[r, 2 * gr + u, c * CHUNK + q0:(c + 1) * CHUNK],
                                        start=True, stop=not diag)
                        if diag:
                            ins = t_.matmul(sbank[:, k % 2, j, q0:q0 + P], identb[:, :], mask_kq[:, :],
                                            start=False, stop=True)
                    ins.then_inc(scores_filled, 1)

                def values(c, k, unit):
                    gr, kt, u, q0 = unit
                    pe.wait_ge(probs_ready, START + i * UNITS + k + 1)
                    if kt == 0 and u == 0:
                        pe.wait_ge(yT4_ready, START + i * NC * GROUPS + c * GROUPS + gr)
                    last = kt == (c + 1) * TPC - 1
                    for j in range(2):
                        h = 4 * gr + 2 * u + j
                        r = 32 * (2 * u + j)
                        ins = t_.matmul(ybank[r:r + 32, q0:CHUNK], vaug[:, kt, h, :], pT[:, k % NPT, j, q0:CHUNK],
                                        start=kt == 0, stop=last)
                    ins.then_inc(probs_used, 1)

                for t in PREP:
                    task(t)
                pe.wait_ge(parts_loaded, START + (i + 1) * NSTACK * 16)
                for k, unit in enumerate(max_units(0)):
                    max_unit(k, unit)
                    side("B", k)
                task(("negmaxT", 0))
                later = max_units(1)
                for c in range(NC):
                    pe.wait_ge(negmax_loaded, START + (i * NC + c + 1) * 2 * 16)
                    units = exp_units(c)
                    base = sum(NU[:c])
                    for n, unit in enumerate(units):
                        scores(c, base + n, unit)
                        if n >= 1:
                            values(c, base + n - 1, units[n - 1])
                        if c == 0:
                            for m in pieces(NM[1], NU[0], n):
                                max_unit(NM[0] + m, later[m])
                        side("CD"[c], n)
                    values(c, base + NU[c] - 1, units[-1])
                    if c == 0:
                        task(("negmaxT", 1))
                for t in TAIL:
                    task(t)


_INS = ['L0_attn_x', 'L0_attn_Wqkv', 'L0_attn_Wproj', 'L0_ffn_Wg', 'L0_ffn_bg', 'L0_ffn_Wu', 'L0_ffn_bu', 'L0_ffn_Wd',
        'L0_ffn_bd', 'L0_ffn_Wq', 'L0_ffn_keys', 'L0_ffn_down_embed', 'L0_ffn_up_embed']


def rope_table():
    inv = np.float32(1.0) / np.float32(10000.0) ** (np.arange(0, DH, 2, dtype=np.float32) / np.float32(DH))
    angle = np.arange(T, dtype=np.float32)[:, None] * inv[None, :].astype(np.float32)
    cos = np.repeat(np.cos(angle), 2, axis=-1)
    sin = np.repeat(np.sin(angle), 2, axis=-1) * np.tile(np.array([-1.0, 1.0], np.float32), DH // 2)
    return np.stack([cos, sin]).astype(np.float32)


def kernel(**inputs):
    import concourse.bacc as bacc
    from concourse.bass_utils import run_bass_kernel_spmd

    nc = bacc.Bacc("TRN2", target_bir_lowering=False, num_devices=1)
    arrays = {f"in_{n}": np.ascontiguousarray(inputs[n]) for n in _INS}
    arrays["rope_table"] = rope_table()
    args = [nc.dram_tensor(n, a.shape, mybir.dt.from_np(a.dtype), kind="ExternalInput").ap()
            for n, a in arrays.items()]
    out = nc.dram_tensor("out_0", (B, T, D), F32, kind="ExternalOutput").ap()
    build(nc, *args, out)
    return run_bass_kernel_spmd(nc, [arrays], core_ids=[0]).results[0]["out_0"]
```

```python
import numpy as np
import concourse.bass as bass
from concourse import mybir
from contextlib import ExitStack

F32 = mybir.dt.float32
BF16 = mybir.dt.bfloat16
ALU = mybir.AluOpType
ACT = mybir.ActivationFunctionType
AX = mybir.AxisListType

START = 1

B, T, D = 4, 1024, 128
H, DH = 16, 8
F = 512
NEXP, NKEYS, RH, KPH = 512, 64, 4, 8
HALF = D // 2
P = 128
NT = T // P
CHUNK = 512
NC = T // CHUNK
TPC = CHUNK // P
NF = F // P
PAIRS = H // 2
GROUPS = H // 4
XI = NEXP // NKEYS
TERMS = [(0, 0), (0, 1), (1, 0), (0, 2), (1, 1), (2, 0)]
KQ = len(TERMS) * DH
ROWS = P // 2
SCALE = float(DH) ** -0.5
MASKED = -1.0e30
EPS = 1e-5
NCAND = 20



def max_units(c):
    units = []
    for i in range(c * TPC, (c + 1) * TPC):
        for k0 in range(0, P * (i + 1), CHUNK):
            w = min(CHUNK, P * (i + 1) - k0)
            n = max(1, CHUNK // w)
            units += [(i, k0, w, list(range(h + e, h + 2 * n, 2))) for h in range(0, H, 2 * n) for e in range(2)]
    return units


def exp_units(c):
    return [(g, kt, u, max(0, kt - c * TPC) * P)
            for g in range(GROUPS) for kt in range((c + 1) * TPC) for u in range(2)]


def next_tasks():
    tasks = [("xT", c) for c in range(NC)]
    for n in range(NT + 1):
        if n < NT:
            tasks.append(("qkv", n))
        if n >= 1:
            tasks.append(("parts", n - 1))
    return tasks + mlp_tasks()


def mlp_tasks():
    tasks = [(kind, c, f) for c in range(NC) for kind in ("down", "gate") for f in range(NF)]
    return tasks + [("up", c, f) for c in range(NC) for f in range(NF)]


NEXT = {t: k for k, t in enumerate(next_tasks())}
NNEXT = len(NEXT)
NMLP = len(mlp_tasks())
READER = {t: "scalar" if t[0] in ("down", "gate") else "vector" for t in NEXT}
NREAD = {e: sum(r == e for r in READER.values()) for e in ("scalar", "vector")}
RETRIEVAL = ("sim", "weights", "zsum", "keep")


def reads(t):
    return sum(READER[u] == READER[t] for u in NEXT if NEXT[u] <= NEXT[t])


def build_slots():
    slots = {}

    def put(phase, step, *tasks):
        slots.setdefault((phase, step), []).extend(tasks)

    for n, stages in enumerate(RETRIEVE_AT):
        for kind, (phase, step) in zip(RETRIEVAL, stages):
            put(phase, step, (kind, n))
    u = [len(exp_units(c)) for c in range(NC)]
    for e in range(NF):
        put("C", 6 + e, ("experts", 0, e))
        put("D", 30 + 3 * e, ("experts", 1, e))
    for g in range(GROUPS):
        at = (g + 1) * u[0] // GROUPS + 1
        put(*(("C", at) if at < u[0] else ("D", 0)), ("ycopy", 0, g))
        put(*(("C", at + 1) if at < u[0] else ("D", 1)), ("y", 0, g))
        at = (g + 1) * u[1] // GROUPS + 1
        put(*(("D", at) if at < u[1] else ("M", 0)), ("ycopy", 1, g))
        put(*(("D", at + 1) if at < u[1] else ("M", 1)), ("y", 1, g))
    put("D", 3, ("yT", 0))
    put("D", 5, ("out", 0))
    put("D", 8, ("outT", 0))
    put("M", 3, ("yT", 1))
    put("M", 5, ("out", 1))
    put("M", 7, ("outT", 1))
    put("D", 0, ("ln",))
    put("D", 3, ("xn", 0), ("xT", 0))
    put("D", 5, ("xn", 1), ("xT", 1))
    for n in range(NT + 1):
        at = 7 + 46 * n // NT
        if n < NT:
            put("D", at, ("qkv", n))
        if n >= 1:
            put("D", at + 1, ("split", n - 1))
            put("D", at + 2, ("parts", n - 1))
    return slots


RETRIEVE_AT = [
    [("M", 9), ("M", 17), ("M", 18), ("B", 6)],
    [("B", 7), ("B", 13), ("B", 14), ("B", 22)],
    [("B", 23), ("B", 29), ("B", 30), ("B", 38)],
    [("B", 39), ("C", 0), ("C", 1), ("C", 4)],
    [("C", 5), ("C", 7), ("C", 8), ("C", 12)],
    [("C", 13), ("C", 15), ("C", 16), ("C", 20)],
    [("C", 21), ("C", 23), ("C", 24), ("C", 28)],
    [("D", 1), ("D", 5), ("D", 6), ("D", 12)],
]
SLOTS = build_slots()
PHASES = [("B", len(max_units(0))), ("C", len(exp_units(0))), ("D", len(exp_units(1))), ("M", NMLP)]
PREPARE = ("ln", "xn", "xT", "qkv", "split", "parts")


def is_next(phase, t):
    return t[0] in PREPARE or phase == "M" and t[0] in RETRIEVAL


class Pass:

    def __init__(self, i, j, base=0):
        self.i, self.j = i, j
        self.base = base
        order = []
        for phase, steps in PHASES:
            for k in range(steps):
                order += [t for t in self.side(phase, k) if t[0] in ("sim", "experts", "y", "yT", "out", "outT")]
            if phase in "BC" and i is not None:
                order.append(("negmaxT", "BC".index(phase)))
        self.work = {t: k for k, t in enumerate(order)}

    def side(self, phase, step):
        return [t for t in SLOTS.get((phase, step), [])
                if (self.j if is_next(phase, t) else self.i) is not None and not (self.i is None and phase != "M")]

    def batch(self, phase, t):
        return self.j if is_next(phase, t) else self.i


FIRST = Pass(None, 0)
NFIRST = len(FIRST.work)
NWORK = len(Pass(0, 1).work)
ALONE = [("ln",), ("xn", 0), ("xT", 0), ("xn", 1), ("xT", 1)]
for _n in range(NT + 1):
    if _n < NT:
        ALONE.append(("qkv", _n))
    if _n >= 1:
        ALONE += [("split", _n - 1), ("parts", _n - 1)]


def loop_pass(i):
    return Pass(i, i + 1, NFIRST + i * NWORK)


LAST = Pass(B - 1, None, NFIRST + (B - 1) * NWORK)


def pieces(total, parts, k):
    return range(total * k // parts, total * (k + 1) // parts)


class Steps:

    def __init__(self, engine, sem, per_pass):
        self.engine, self.sem, self.per, self.base, self.n, self.first = engine, sem, per_pass, 0, 0, 0

    def begin(self, p):
        if p.i is not None:
            self.first = self.first or self.n
            self.base = self.first + p.i * self.per
        self.n = 0

    def mark(self, ins):
        ins.then_inc(self.sem, 1)
        self.n += 1
        return self.n

    def need(self, n):
        self.engine.wait_ge(self.sem, START + self.base + n)

    def end(self, p):
        if p.i is not None:
            assert self.n == (self.per if p.j is not None else self.per - self.first), (self.n, self.per, self.first)


def build(nc, x, wqkv, wproj, wg, bg, wu, bu, wd, bd, wq, keys, down, up, rope, out):
    ctx = ExitStack()
    with ctx:
        def sb(name, shape, dt=F32):
            return ctx.enter_context(nc.sbuf_tensor(name, shape, dt))

        def sem(name):
            return ctx.enter_context(nc.semaphore(name))

        parts_dram = nc.dram_tensor("parts_scratch", (2, 3, P, T), BF16, kind="Internal").ap()
        negmax_dram = nc.dram_tensor("negmax_scratch", (2, 3, PAIRS, T), BF16, kind="Internal").ap()

        ident = sb("ident", [P, P])
        identb = sb("identb", [P, P], BF16)
        mask_qk = sb("mask_qk", [P, P], BF16)
        mask_kq = sb("mask_kq", [P, P], BF16)
        rope_sb = sb("rope_sb", [P, 2, NT, DH])
        wqkv_sb = sb("wqkv_sb", [P, 3 * D])
        wproj_sb = sb("wproj_sb", [P, D])
        wg_sb = sb("wg_sb", [P, F])
        wu_sb = sb("wu_sb", [P, F])
        wd_sb = sb("wd_sb", [P, NF, D])
        up_sb = sb("up_sb", [P, NF, D])
        downT = sb("downT", [P, NEXP])
        wsim = sb("wsim", [P, 2, RH, NKEYS])
        bg_sb = sb("bg_sb", [P, NF])
        bu_sb = sb("bu_sb", [P, NF])
        bd_sb = sb("bd_sb", [P, 1])
        half_neg = sb("half_neg", [P, NT])
        eps = sb("eps", [P, NT])
        zero_rows = sb("zero_rows", [3, 1, T], BF16)
        carrier = sb("carrier", [P, 1])
        wq_sb = sb("wq_sb", [P, RH, 2, HALF])
        keys_sb = sb("keys_sb", [NKEYS, RH, 2, HALF])
        down_sb = sb("down_sb", [P, NF, D])
        wqT = sb("wqT", [P, P])
        keysT = sb("keysT", [P, NKEYS])

        xin = sb("xin", [P, NT, D])
        stats = sb("stats", [P, NT, 6])
        meanvar = sb("meanvar", [P, NT, 2])
        vareps = sb("vareps", [P, NT])
        rstd = sb("rstd", [P, NT])
        xn = sb("xn", [P, NT, D])
        xnT_next = sb("xnT_next", [P, T])
        xnT = sb("xnT", [P, T])
        qk = sb("qk", [P, 2, 2 * H, DH])
        rot_a = sb("rot_a", [P, 2 * H, DH])
        rot_b = sb("rot_b", [P, 2 * H, DH])
        rot = sb("rot", [P, 2, 2 * H, DH])
        rest = sb("rest", [P, 2 * D])
        parts = sb("parts", [P, 2, 3, 2 * D], BF16)
        partsT = sb("partsT", [P, 2, 3, T], BF16)
        qs = sb("qs", [P, PAIRS, T], BF16)
        ks = sb("ks", [P, PAIRS, T], BF16)
        VW = (H - 1) * (DH + 1) + 32
        vaug = sb("vaug", [P, NT, VW])
        vaug_next = sb("vaug_next", [P, NT, VW])
        vheads = vaug_next[:, :, 0:H * (DH + 1)].rearrange("p n (h d) -> p n h d", d=DH + 1)

        pmax = sb("pmax", [P, NT, 2, H])
        rmax = sb("rmax", [P, TPC, H])
        mrest = sb("mrest", [P, TPC, H])
        negmax_pad = sb("negmax_pad", [P, TPC, P], BF16)
        negmax = negmax_pad[:, :, 0:3 * H].rearrange("p n (e s j) -> p n e s j", e=2, s=3)
        negmaxT = sb("negmaxT", [3 * H, CHUNK], BF16)
        NPT = 4
        pT = sb("pT", [P, NPT, 2, CHUNK])
        yT4 = sb("yT4", [P, CHUNK])
        ytm = sb("ytm", [P, TPC, H, DH])
        yinv = sb("yinv", [P, TPC, 4])
        yT = sb("yT", [P, CHUNK])

        sgate = sb("sgate", [P, NC, NF, CHUNK])
        hT = sgate
        sexp = sb("sexp", [P, NC, NF, CHUNK])
        gT = sexp
        sim = sb("sim", [P, 2 * RH, NKEYS])
        simx = sb("simx", [P, RH, XI])
        top = sb("top", [P, 2 * RH, KPH])
        cand = sb("cand", [P, RH, NCAND])
        best = sb("best", [P, RH, KPH])
        ND = RH * (KPH + XI + NKEYS)
        dif = sb("dif", [P, ND])
        edif = sb("edif", [P, ND])
        zsum = sb("zsum", [P, RH])
        zinv = sb("zinv", [P, RH])
        exz = sb("exz", [P, RH, XI])
        ssum = sb("ssum", [P, RH, XI, NKEYS])
        wsum = sb("wsum", [P, RH, XI * NKEYS])
        coef4 = wsum
        inside = sb("inside", [P, RH])
        inside1 = sb("inside1", [P, 1])
        clipped = sb("clipped", [P, 1])
        coef = sb("coef", [P, TPC, NEXP])
        oT = sb("oT", [P, CHUNK])
        xres = sb("xres", [P, TPC, D])
        osb = sb("osb", [P, TPC, D])

        work = ctx.enter_context(nc.psum_tensor("work", [P, CHUNK], F32))
        mbank = ctx.enter_context(nc.psum_tensor("mbank", [P, 2, CHUNK], F32))
        sbank = ctx.enter_context(nc.psum_tensor("sbank", [P, 2, 2, CHUNK], F32))
        ybank = ctx.enter_context(nc.psum_tensor("ybank", [P, CHUNK], F32))
        workb = work[:, :].bitcast(BF16)
        mbankb = [mbank[:, k, :].bitcast(BF16) for k in range(2)]

        weights_loaded = sem("weights_loaded")
        consts_made = sem("consts_made")
        pool_setup = sem("pool_setup")
        setup_filled = sem("setup_filled")
        setup_copied = sem("setup_copied")
        x_loaded = sem("x_loaded")
        res_loaded = sem("res_loaded")
        stats_done = sem("stats_done")
        var_ready = sem("var_ready")
        rstd_ready = sem("rstd_ready")
        xn_ready = sem("xn_ready")
        work_filled = sem("work_filled")
        work_copied = sem("work_copied")
        qk_copied = sem("qk_copied")
        rot_ready = sem("rot_ready")
        parts_ready = sem("parts_ready")
        parts_stored = sem("parts_stored")
        parts_loaded = sem("parts_loaded")
        xnT_moved = sem("xnT_moved")
        v_moved = sem("v_moved")
        next_filled = sem("next_filled")
        next_read_scalar = sem("next_read_scalar")
        next_read_vector = sem("next_read_vector")
        max_filled = sem("max_filled")
        max_read = sem("max_read")
        negmax_ready = sem("negmax_ready")
        negmax_stored = sem("negmax_stored")
        negmax_loaded = sem("negmax_loaded")
        scores_filled = sem("scores_filled")
        probs_ready = sem("probs_ready")
        probs_used = sem("probs_used")
        yT4_ready = sem("yT4_ready")
        dif_ready = sem("dif_ready")
        edif_ready = sem("edif_ready")
        zinv_ready = sem("zinv_ready")
        pairs_ready = sem("pairs_ready")
        weighed = sem("weighed")
        clipped_ready = sem("clipped_ready")
        kept_ready = sem("kept_ready")
        coef_ready = sem("coef_ready")
        out_stored = sem("out_stored")
        pool_steps = sem("pool_steps")
        dve_steps = sem("dve_steps")

        block = ctx.enter_context(nc.Block())
        x_v = x.rearrange("b (n p) d -> b p n d", p=P)
        o_v = out.rearrange("b (n p) d -> b p n d", p=P)
        NLOAD = 15
        NCONST = 11
        NSTACK = (len(TERMS) * 2 + 1) * 2

        NU = [len(exp_units(c)) for c in range(NC)]
        NM = [len(max_units(c)) for c in range(NC)]
        UNITS, MUNITS = sum(NU), sum(NM)
        PRODS = UNITS // 2
        SETUP = [downT[:, t * P:(t + 1) * P] for t in range(NF)]
        for h in range(RH):
            SETUP += [wqT[:, :], keysT[:, :], wsim[:, 0, h, :], wsim[:, 1, h, :]]

        def filled(e, p, t):
            e.wait_ge(work_filled, START + p.base + p.work[t] + 1)

        def copied(e, p, t):
            e.wait_ge(work_copied, START + p.base + p.work[t] + 1)

        def filled_before(e, p, t=None):
            e.wait_ge(work_filled, START + p.base + (p.work[t] + 1 if t else 0))

        def next_ready(e, b, t):
            e.wait_ge(next_filled, START + b * NNEXT + NEXT[t] + 1)

        def next_bank(t):
            return NEXT[t] % 2

        @block.sync
        def _(sp):
            for dst, src in [
                (wqkv_sb[:, :], wqkv), (wproj_sb[:, :], wproj), (wg_sb[:, :], wg), (wu_sb[:, :], wu),
                (wd_sb[:, :, :], wd.rearrange("(t p) c -> p t c", p=P)),
                (up_sb[:, :, :], up.rearrange("(t p) c -> p t c", p=P)),
                (down_sb[:, :, :], down.rearrange("(t p) c -> p t c", p=P)),
                (wq_sb[:, :, 0, :], wq[:, 0:RH * HALF].rearrange("d (h n) -> d h n", h=RH)),
                (wq_sb[:, :, 1, :], wq[:, RH * HALF:].rearrange("d (h n) -> d h n", h=RH)),
                (keys_sb[:, :, :, :], keys.rearrange("h k a n -> k h a n")),
                (bg_sb[:, :], bg.rearrange("(t p) -> p t", p=P)),
                (bu_sb[:, :], bu.rearrange("(t p) -> p t", p=P)),
                (bd_sb[:, :], bd.rearrange("(p a) -> p a", a=1)),
                (rope_sb[:, 0, :, :], rope[0].rearrange("(n p) d -> p n d", p=P)),
                (rope_sb[:, 1, :, :], rope[1].rearrange("(n p) d -> p n d", p=P)),
            ]:
                sp.dma_start(dst, src, allow_slow_non_contiguous=True).then_inc(weights_loaded, 16)

            for s in (x_loaded, res_loaded, parts_stored, parts_loaded, negmax_stored, negmax_loaded,
                      out_stored, xnT_moved, v_moved):
                sp.sem_inc(s, START)
            def load_rows(dst, batch, n0, n1, loaded):
                sp.dma_start(dst, batch[:, :, n0:n1, :].rearrange("b p n d -> (b p) n d")).then_inc(loaded, 16)

            def run(p, rows, next_rows, out_rows):
                i, j = p.i, p.j
                if j is not None:
                    sp.wait_ge(xn_ready, START + j * NT)
                    load_rows(xin[:, :, :], next_rows, 0, NT, x_loaded)
                if i is not None:
                    sp.wait_ge(work_copied, START + p.base)
                    load_rows(xres[:, :, :], rows, 0, TPC, res_loaded)
                    for c in range(NC):
                        cols = slice(c * CHUNK, (c + 1) * CHUNK)
                        copied(sp, p, ("negmaxT", c))
                        sp.dma_start(negmax_dram.rearrange("h s j t -> (h s j) t")[:, cols], negmaxT[:, :])\
                            .then_inc(negmax_stored, 16)
                        sp.wait_ge(negmax_stored, START + (i * NC + c + 1) * 16)
                        for hh in range(2):
                            r = HALF * hh + KQ
                            sp.dma_start(qs[r:r + 3, :, cols], negmax_dram[hh][:, :, cols])\
                                .then_inc(negmax_loaded, 16)
                    copied(sp, p, ("outT", 0))
                    sp.dma_start(out_rows[:, :, 0:TPC, :].rearrange("b p n d -> (b p) n d"), osb[:, :, :])\
                        .then_inc(out_stored, 16)
                    load_rows(xres[:, :, :], rows, TPC, NT, res_loaded)
                if j is not None:
                    sp.wait_ge(next_read_vector, START + j * NREAD["vector"] + reads(("parts", NT - 1)))
                    for s in range(3):
                        for a in range(2):
                            sp.dma_start(parts_dram[a, s], partsT[:, a, s, :]).then_inc(parts_stored, 16)
                    sp.wait_ge(scores_filled, START + j * UNITS)
                    sp.dma_start(xnT[:, :], xnT_next[:, :]).then_inc(xnT_moved, 16)
                    sp.wait_ge(parts_stored, START + (j + 1) * (6 * 16))
                    for t, pair in enumerate(TERMS):
                        for a, dst in ((0, qs), (1, ks)):
                            for hh in range(2):
                                src = parts_dram[a, pair[a]].rearrange("(j h d) t -> h d j t", h=2, d=DH)[hh]
                                r = HALF * hh + DH * t
                                sp.dma_start(dst[r:r + DH, :, :], src).then_inc(parts_loaded, 16)
                    for hh in range(2):
                        r = HALF * hh + KQ
                        sp.dma_start(qs[r:r + 3, :, :], zero_rows[:, :, :].to_broadcast([3, PAIRS, T])).then_inc(parts_loaded, 16)
                    sp.wait_ge(probs_used, START + j * PRODS)
                    sp.dma_start(vaug[:, :, :], vaug_next[:, :, :]).then_inc(v_moved, 16)
                if i is not None:
                    copied(sp, p, ("outT", 1))
                    sp.dma_start(out_rows[:, :, TPC:NT, :].rearrange("b p n d -> (b p) n d"), osb[:, :, :])\
                        .then_inc(out_stored, 16)

            run(FIRST, None, x_v[0:1], None)
            with sp.Fori(0, B - 1) as i:
                run(loop_pass(i), x_v[bass.ds(i, 1)], x_v[bass.ds(i + 1, 1)], o_v[bass.ds(i, 1)])
            run(LAST, x_v[B - 1:B], None, o_v[B - 1:B])
            sp.wait_ge(out_stored, START + B * NC * 16)

        @block.gpsimd
        def _(pool):
            g = nc.gpsimd
            for m in (ident, identb, mask_qk, mask_kq):
                g.memset(m[:, :], 0.0).then_inc(pool_setup, 1)
            pool.wait_ge(pool_setup, 4)
            for m in (ident, identb):
                g.affine_select(out=m[:, :], in_=m[:, :], pattern=[[-1, P]], compare_op=ALU.not_equal, fill=1.0,
                                base=0, channel_multiplier=1).then_inc(consts_made, 1)
            g.affine_select(out=mask_qk[:, :], in_=mask_qk[:, :], pattern=[[-1, P]], compare_op=ALU.is_ge,
                            fill=MASKED, base=0, channel_multiplier=1).then_inc(consts_made, 1)
            g.affine_select(out=mask_kq[:, :], in_=mask_kq[:, :], pattern=[[1, P]], compare_op=ALU.is_ge,
                            fill=MASKED, base=0, channel_multiplier=-1).then_inc(consts_made, 1)
            g.memset(half_neg[:, :], -0.5).then_inc(consts_made, 1)
            g.memset(eps[:, :], EPS).then_inc(consts_made, 1)
            g.memset(negmax_pad[:, :, :], 0.0).then_inc(consts_made, 1)
            g.memset(ks[:, :, :], 1.0).then_inc(consts_made, 1)
            g.memset(qs[:, :, :], 0.0).then_inc(consts_made, 1)
            g.memset(zero_rows[:, :, :], 0.0).then_inc(consts_made, 1)
            g.memset(vaug_next[:, :, :], 0.0).then_inc(pool_setup, 1)
            pool.wait_ge(pool_setup, 5)
            g.memset(vheads[:, :, :, DH:DH + 1], 1.0).then_inc(consts_made, 1)
            pool.wait_ge(weights_loaded, 16 * NLOAD)
            pool.wait_ge(consts_made, NCONST)
            for s in (var_ready, rstd_ready, rot_ready, pairs_ready, weighed, coef_ready, pool_steps):
                pool.sem_inc(s, START)
            steps = Steps(pool, pool_steps, 6 * NT)

            def task(p, phase, t):
                kind, n, b = t[0], t[-1], p.batch(phase, t)
                if kind == "ln":
                    pool.wait_ge(stats_done, START + (b + 1) * NT)
                    pool.wait_ge(xn_ready, START + b * NT)
                    g.tensor_tensor(vareps[:, :], meanvar[:, :, 1], eps[:, :], ALU.add).then_inc(var_ready, 1)
                    pool.wait_ge(var_ready, START + b + 1)
                    g.tensor_tensor(rstd[:, :], vareps[:, :], half_neg[:, :], ALU.pow).then_inc(rstd_ready, 1)
                elif kind == "qkv":
                    pool.wait_ge(qk_copied, START + b * NT + n + 1)
                    q = qk[:, n % 2, :, :]
                    cos = rope_sb[:, 0, n:n + 1, :].to_broadcast([P, 2 * H, DH])
                    sin = rope_sb[:, 1, n:n + 1, :].rearrange("p o (e t) -> p o e t", t=2)
                    a2 = q.rearrange("p h (e t) -> p h e t", t=2)
                    b2 = rot_b[:, :, :].rearrange("p h (e t) -> p h e t", t=2)
                    steps.mark(g.tensor_tensor(rot_a[:, :, :], q, cos, ALU.mult))
                    for e in range(2):
                        k = steps.mark(g.tensor_tensor(b2[:, :, :, e], a2[:, :, :, 1 - e],
                                                       sin[:, :, :, e].to_broadcast([P, 2 * H, DH // 2]), ALU.mult))
                    steps.need(k)
                    pool.wait_ge(parts_ready, START + b * NT + max(n - 1, 0))
                    g.tensor_tensor(rot[:, n % 2, :, :], rot_a[:, :, :], rot_b[:, :, :], ALU.add)\
                        .then_inc(rot_ready, 1)
                    pool.wait_ge(rot_ready, START + b * NT + n + 1)
                elif kind == "sim":
                    copied(pool, p, ("sim", n))
                    pool.wait_ge(kept_ready, START + (b * NT + n) * RH)
                    for h in range(RH):
                        g.tensor_tensor(ssum[:, h, :, :],
                                        sim[:, h, 0:XI].unsqueeze(2).to_broadcast([P, XI, NKEYS]),
                                        sim[:, RH + h:RH + h + 1, :].to_broadcast([P, XI, NKEYS]), ALU.add)\
                            .then_inc(pairs_ready, 1)
                elif kind == "zsum":
                    pool.wait_ge(zinv_ready, START + b * NT + n + 1)
                    k = steps.mark(g.tensor_tensor(
                        exz[:, :, :], edif[:, RH * KPH:RH * (KPH + XI)].rearrange("p (h i) -> p h i", h=RH),
                        zinv[:, :].unsqueeze(2).to_broadcast([P, RH, XI]), ALU.mult))
                    steps.need(k)
                    ey = edif[:, RH * (KPH + XI):].rearrange("p (h j) -> p h j", h=RH)
                    for h in range(RH):
                        g.tensor_tensor(wsum[:, h, :].rearrange("p (i j) -> p i j", i=XI),
                                        exz[:, h, :].unsqueeze(2).to_broadcast([P, XI, NKEYS]),
                                        ey[:, h:h + 1, :].to_broadcast([P, XI, NKEYS]), ALU.mult)\
                            .then_inc(weighed, 1)
                elif kind == "keep":
                    pool.wait_ge(kept_ready, START + (b * NT + n + 1) * RH)
                    k = steps.mark(g.tensor_tensor(coef4[:, 0:2, :], coef4[:, 0:2, :], coef4[:, 2:4, :], ALU.add))
                    steps.need(k)
                    filled_before(pool, p, ("experts", n // TPC - 1, NF - 1) if n >= TPC else None)
                    c = n % TPC
                    pool.wait_ge(clipped_ready, START + b * NT + n + 1)
                    k = steps.mark(g.tensor_tensor(coef[:, c, :], coef4[:, 0, :], coef4[:, 1, :], ALU.add))
                    steps.need(k)
                    g.tensor_tensor(coef[:, c, NEXP - 1:NEXP], coef[:, c, NEXP - 1:NEXP], clipped[:, :], ALU.add)\
                        .then_inc(coef_ready, 1)
                    pool.wait_ge(coef_ready, START + b * NT + n + 1)

            def run(p):
                steps.begin(p)
                if p is FIRST:
                    for t in ALONE:
                        task(p, "D", t)
                for phase, count in PHASES:
                    for k in range(count):
                        for t in p.side(phase, k):
                            task(p, phase, t)
                steps.end(p)

            run(FIRST)
            with pool.Fori(0, B - 1) as i:
                run(loop_pass(i))
            run(LAST)

        @block.scalar
        def _(act):
            a = nc.scalar
            for n, dst in enumerate(SETUP):
                act.wait_ge(setup_filled, n + 1)
                a.activation(dst, work[:, 0:dst.shape[-1]], ACT.Copy).then_inc(setup_copied, 1)
            act.wait_ge(weights_loaded, 16 * NLOAD)
            act.wait_ge(consts_made, NCONST)
            for s in (yT4_ready, edif_ready, probs_ready, next_read_scalar, work_copied):
                act.sem_inc(s, START)
            def task(p, phase, t):
                kind, b = t[0], p.batch(phase, t)
                if kind in ("negmaxT", "sim", "yT", "out"):
                    filled(act, p, t)
                if kind == "negmaxT":
                    act.wait_ge(negmax_stored, START + (b * NC + t[1]) * 16)
                    a.activation(negmaxT[:, :], workb[0:3 * H, 0:CHUNK], ACT.Copy).then_inc(work_copied, 1)
                elif kind == "sim":
                    n = t[1]
                    act.wait_ge(dif_ready, START + b * NT + n)
                    act.wait_ge(pairs_ready, START + (b * NT + n) * RH)
                    a.activation(sim[:, :, :], work[:, :].rearrange("p (g k) -> p g k", k=NKEYS), ACT.Copy)\
                        .then_inc(work_copied, 1)
                elif kind == "weights":
                    n = t[1]
                    act.wait_ge(dif_ready, START + b * NT + n + 1)
                    act.wait_ge(weighed, START + (b * NT + n) * RH)
                    a.activation(edif[:, :], dif[:, :], ACT.Exp).then_inc(edif_ready, 1)
                elif kind == "ycopy":
                    k = t[1] * GROUPS + t[2]
                    act.wait_ge(probs_used, START + b * PRODS + (sum(NU[:t[1]]) + (t[2] + 1) * NU[t[1]] // GROUPS) // 2)
                    filled_before(act, p, ("y", (k - 1) // GROUPS, (k - 1) % GROUPS) if k else None)
                    a.activation(yT4[:, :], ybank[:, :], ACT.Copy).then_inc(yT4_ready, 1)
                elif kind == "yT":
                    a.activation(yT[:, :], work[:, :], ACT.Copy).then_inc(work_copied, 1)
                elif kind == "out":
                    a.activation(oT[:, :], work[:, :], ACT.Identity, bias=bd_sb[:, 0:1]).then_inc(work_copied, 1)

            def silu(p, t):
                kind, c, f = t
                if p.i is not None:
                    filled_before(act, p, ("out", c))
                next_ready(act, p.j, t)
                src = mbank[:, next_bank(t), :]
                if kind == "down":
                    a.activation(sexp[:, c, f, :], src, ACT.Silu).then_inc(next_read_scalar, 1)
                else:
                    a.activation(sgate[:, c, f, :], src, ACT.Silu, bias=bg_sb[:, f:f + 1])\
                        .then_inc(next_read_scalar, 1)

            def exponentials(p, c, n):
                gr, kt, u, q0 = exp_units(c)[n]
                k = sum(NU[:c]) + n
                act.wait_ge(scores_filled, START + p.i * UNITS + k + 1)
                act.wait_ge(probs_used, START + p.i * PRODS + max(k // 2 + 1 - NPT // 2, 0))
                a.activation(pT[:, k % NPT, :, q0:CHUNK], sbank[:, k % 2, :, q0:CHUNK], ACT.Exp,
                             scale=SCALE).then_inc(probs_ready, 1)

            def run(p):
                for phase, count in PHASES:
                    for k in range(count):
                        if phase in "CD" and p.i is not None:
                            exponentials(p, "CD".index(phase), k)
                        if phase == "M" and p.j is not None and READER[mlp_tasks()[k]] == "scalar":
                            silu(p, mlp_tasks()[k])
                        for t in p.side(phase, k):
                            task(p, phase, t)
                    if phase in "BC" and p.i is not None:
                        task(p, phase, ("negmaxT", "BC".index(phase)))

            run(FIRST)
            with act.Fori(0, B - 1) as i:
                run(loop_pass(i))
            run(LAST)

        @block.vector
        def _(dve):
            v = nc.vector
            TOP_STEPS = 1 + 2 * RH + 4 + 2 + RH + 2
            steps = Steps(dve, dve_steps, NT + 3 * NT + (1 + 3) + (2 + 3) + NT * TOP_STEPS + NC * GROUPS)
            dve.wait_ge(weights_loaded, 16 * NLOAD)
            for s in (stats_done, xn_ready, qk_copied, parts_ready, max_read, negmax_ready, dif_ready,
                      zinv_ready, kept_ready, clipped_ready, next_read_vector, dve_steps):
                dve.sem_inc(s, START)

            def best_pairs(p, b, n):
                copied(dve, p, ("sim", n))
                dve.wait_ge(kept_ready, START + (b * NT + n) * RH)
                steps.mark(v.tensor_copy(simx[:, :, :], sim[:, 0:RH, 0:XI]))
                for a in range(2 * RH):
                    k = steps.mark(v.max(top[:, a, :], sim[:, a, :]))
                steps.need(k)
                xs, ys = top[:, 0:RH, :], top[:, RH:2 * RH, :]

                def wide(ap, w):
                    return ap.to_broadcast([P, RH, w])

                steps.mark(v.tensor_tensor(cand[:, :, 0:8], ys, wide(xs[:, :, 0:1], 8), ALU.add))
                steps.mark(v.tensor_tensor(cand[:, :, 8:12], ys[:, :, 0:4], wide(xs[:, :, 1:2], 4), ALU.add))
                steps.mark(v.tensor_tensor(cand[:, :, 12:16].rearrange("p h (a b) -> p h a b", a=2),
                                           ys[:, :, 0:2].unsqueeze(2).to_broadcast([P, RH, 2, 2]),
                                           xs[:, :, 2:4].unsqueeze(3).to_broadcast([P, RH, 2, 2]), ALU.add))
                k = steps.mark(v.tensor_tensor(cand[:, :, 16:20], xs[:, :, 4:8], wide(ys[:, :, 0:1], 4),
                                               ALU.add))
                dve.wait_ge(edif_ready, START + b * NT + n)
                steps.need(k)
                o = RH * KPH
                steps.mark(v.tensor_tensor(dif[:, o:o + RH * XI].rearrange("p (h i) -> p h i", h=RH),
                                           simx[:, :, :], wide(xs[:, :, 0:1], XI), ALU.subtract))
                o += RH * XI
                steps.mark(v.tensor_tensor(dif[:, o:].rearrange("p (h j) -> p h j", h=RH),
                                           sim[:, RH:2 * RH, :], wide(ys[:, :, 0:1], NKEYS), ALU.subtract))
                for h in range(RH):
                    k = steps.mark(v.max(best[:, h, :], cand[:, h, :]))
                steps.need(k)
                v.tensor_tensor(dif[:, 0:RH * KPH].rearrange("p (h r) -> p h r", h=RH), best[:, :, :],
                                wide(best[:, :, 0:1], KPH), ALU.subtract).then_inc(dif_ready, 1)

            def weight_sums(b, n):
                dve.wait_ge(edif_ready, START + b * NT + n + 1)
                k = steps.mark(v.tensor_reduce(zsum[:, :],
                                               edif[:, 0:RH * KPH].rearrange("p (h r) -> p h r", h=RH),
                                               axis=AX.X, op=ALU.add))
                steps.need(k)
                dve.wait_ge(weighed, START + (b * NT + n) * RH)
                v.reciprocal(zinv[:, :], zsum[:, :]).then_inc(zinv_ready, 1)

            def keep_best(b, n):
                dve.wait_ge(coef_ready, START + b * NT + n)
                for h in range(RH):
                    dve.wait_ge(weighed, START + (b * NT + n) * RH + h + 1)
                    v.scalar_tensor_tensor(out=coef4[:, h, :], in0=ssum[:, h, :, :].rearrange("p i j -> p (i j)"),
                                           scalar=best[:, h, KPH - 1:KPH], in1=wsum[:, h, :],
                                           op0=ALU.is_ge, op1=ALU.mult, accum_out=inside[:, h:h + 1])\
                        .then_inc(kept_ready, 1)
                dve.wait_ge(kept_ready, START + (b * NT + n + 1) * RH)
                k = steps.mark(v.tensor_reduce(inside1[:, :], inside[:, :], axis=AX.X, op=ALU.add))
                steps.need(k)
                v.tensor_scalar(clipped[:, :], inside1[:, :], -1.0, float(RH), ALU.mult, ALU.add)\
                    .then_inc(clipped_ready, 1)

            def prepare(b, t):
                kind, n = t[0], t[-1]
                if kind == "ln":
                    dve.wait_ge(x_loaded, START + 16 * (b + 1))
                    for n in range(NT):
                        k = steps.mark(v.bn_stats(stats[:, n, :], xin[:, n, :]))
                    steps.need(k)
                    v.memset(carrier[:, :], 0.0)
                    for n in range(NT):
                        v.bn_aggr(meanvar[:, n, :], stats[:, n, :]).then_inc(stats_done, 1)
                elif kind == "xn":
                    dve.wait_ge(stats_done, START + (b + 1) * NT)
                    dve.wait_ge(rstd_ready, START + b + 1)
                    dve.wait_ge(next_filled, START + b * NNEXT)
                    for m in range(n * TPC, (n + 1) * TPC):
                        v.tensor_scalar(xn[:, m, :], xin[:, m, :], meanvar[:, m, 0:1], rstd[:, m:m + 1],
                                        ALU.subtract, ALU.mult).then_inc(xn_ready, 1)
                elif kind == "xT":
                    dve.wait_ge(xnT_moved, START + 16 * b)
                    next_ready(dve, b, t)
                    v.tensor_copy(xnT_next[:, n * CHUNK:(n + 1) * CHUNK], mbank[:, next_bank(t), :])\
                        .then_inc(next_read_vector, 1)
                elif kind == "qkv":
                    next_ready(dve, b, t)
                    dve.wait_ge(rot_ready, START + b * NT + max(n - 1, 0))
                    src = mbank[:, next_bank(t), :]
                    v.tensor_copy(qk[:, n % 2, :, :], src[:, 0:2 * D].rearrange("p (h d) -> p h d", d=DH))\
                        .then_inc(qk_copied, 1)
                    dve.wait_ge(v_moved, START + 16 * b)
                    v.tensor_copy(vheads[:, n, :, 0:DH], src[:, 2 * D:3 * D].rearrange("p (h d) -> p h d", d=DH))\
                        .then_inc(next_read_vector, 1)
                elif kind == "split":
                    dve.wait_ge(rot_ready, START + b * NT + n + 1)
                    if n >= 2:
                        next_ready(dve, b, ("parts", n - 2))
                    r = rot[:, n % 2, :, :].rearrange("p h d -> p (h d)")
                    pt = parts[:, n % 2, :, :]
                    k = steps.mark(v.tensor_copy(pt[:, 0, :], r))
                    steps.need(k)
                    k = steps.mark(v.tensor_tensor(rest[:, :], r, pt[:, 0, :], ALU.subtract))
                    steps.need(k)
                    k = steps.mark(v.tensor_copy(pt[:, 1, :], rest[:, :]))
                    steps.need(k)
                    v.tensor_tensor(pt[:, 2, :], rest[:, :], pt[:, 1, :], ALU.subtract).then_inc(parts_ready, 1)
                    dve.wait_ge(parts_ready, START + b * NT + n + 1)
                elif kind == "parts":
                    dve.wait_ge(parts_stored, START + b * (6 * 16))
                    next_ready(dve, b, t)
                    v.tensor_copy(partsT[:, :, :, n * P:(n + 1) * P].rearrange("p a s t -> p (a s) t"),
                                  mbankb[next_bank(t)][:, 0:6 * P].rearrange("p (a t) -> p a t", t=P))\
                        .then_inc(next_read_vector, 1)

            def up_product(b, t):
                _, c, f = t
                next_ready(dve, b, t)
                v.scalar_tensor_tensor(out=hT[:, c, f, :], in0=mbank[:, next_bank(t), :], scalar=bu_sb[:, f:f + 1],
                                       in1=sgate[:, c, f, :], op0=ALU.add, op1=ALU.mult)\
                    .then_inc(next_read_vector, 1)

            def task(p, phase, t):
                kind, b = t[0], p.batch(phase, t)
                if kind in PREPARE:
                    prepare(b, t)
                if kind in ("experts", "y", "outT"):
                    filled(dve, p, t)
                if kind == "experts":
                    v.tensor_tensor(gT[:, t[1], t[2], :], work[:, :], sexp[:, t[1], t[2], :], ALU.mult)\
                        .then_inc(work_copied, 1)
                elif kind == "y":
                    gr = t[2]
                    wv = work[:, :].rearrange("p (n j d) -> p n j d", n=TPC, j=4)
                    k = steps.mark(v.reciprocal(yinv[:, :, :], wv[:, :, :, DH]))
                    steps.need(k)
                    v.tensor_tensor(ytm[:, :, 4 * gr:4 * gr + 4, :], wv[:, :, :, 0:DH],
                                    yinv[:, :, :].unsqueeze(3).to_broadcast([P, TPC, 4, DH]), ALU.mult)\
                        .then_inc(work_copied, 1)
                elif kind == "outT":
                    c = t[1]
                    dve.wait_ge(res_loaded, START + 16 * (b * NC + c + 1))
                    dve.wait_ge(out_stored, START + 16 * (b * NC + c))
                    v.tensor_tensor(osb[:, :, :], work[:, :].rearrange("p (n d) -> p n d", d=D), xres[:, :, :],
                                    ALU.add).then_inc(work_copied, 1)
                elif kind == "sim":
                    best_pairs(p, b, t[1])
                elif kind == "zsum":
                    weight_sums(b, t[1])
                elif kind == "keep":
                    keep_best(b, t[1])

            def max_unit(i, k, unit):
                it, k0, w, heads = unit
                dve.wait_ge(max_filled, START + i * MUNITS + k + 1)
                v.tensor_reduce(pmax[:, it, k0 // CHUNK, heads[0]:heads[-1] + 1:2],
                                mbank[:, k % 2, 0:w * len(heads)].rearrange("p (h w) -> p h w", w=w),
                                axis=AX.X, op=ALU.max).then_inc(max_read, 1)

            def negated(p, c):
                dve.wait_ge(max_read, START + p.i * MUNITS + sum(NM[:c + 1]))
                n = slice(c * TPC, (c + 1) * TPC)
                m = pmax[:, n, 0, :]
                if c > 0:
                    k = steps.mark(v.tensor_tensor(mrest[:, :, :], m, pmax[:, n, 1, :], ALU.max))
                    steps.need(k)
                    m = mrest[:, :, :]
                k = steps.mark(v.tensor_scalar(rmax[:, :, :], m, -1.0, None, ALU.mult))
                steps.need(k)
                filled_before(dve, p, ("negmaxT", c - 1) if c else None)
                pj = [ap.rearrange("p n (j e) -> p n e j", e=2) for ap in (rmax[:, :, :], mrest[:, :, :])]
                k = steps.mark(v.tensor_copy(negmax[:, :, :, 0, :], pj[0]))
                steps.need(k)
                k = steps.mark(v.tensor_tensor(pj[1], pj[0], negmax[:, :, :, 0, :], ALU.subtract))
                steps.need(k)
                k = steps.mark(v.tensor_copy(negmax[:, :, :, 1, :], pj[1]))
                steps.need(k)
                v.tensor_tensor(negmax[:, :, :, 2, :], pj[1], negmax[:, :, :, 1, :], ALU.subtract)\
                    .then_inc(negmax_ready, 1)

            later = max_units(1)

            def run(p):
                steps.begin(p)
                if p is FIRST:
                    for t in ALONE:
                        task(p, "D", t)
                for phase, count in PHASES:
                    for k in range(count):
                        if phase == "B" and p.i is not None:
                            max_unit(p.i, k, max_units(0)[k])
                        if phase == "C" and p.i is not None:
                            for m in pieces(NM[1], NU[0], k):
                                max_unit(p.i, NM[0] + m, later[m])
                        if phase == "M" and p.j is not None and READER[mlp_tasks()[k]] == "vector":
                            up_product(p.j, mlp_tasks()[k])
                        for t in p.side(phase, k):
                            task(p, phase, t)
                    if phase in "BC" and p.i is not None:
                        negated(p, "BC".index(phase))
                steps.end(p)

            run(FIRST)
            with dve.Fori(0, B - 1) as i:
                run(loop_pass(i))
            run(LAST)

        @block.tensor
        def _(pe):
            t_ = nc.tensor
            pe.wait_ge(weights_loaded, 16 * NLOAD)
            pe.wait_ge(consts_made, NCONST)
            n = 0

            def setup_done(ins):
                nonlocal n
                ins.then_inc(setup_filled, 1)
                n += 1
                pe.wait_ge(setup_copied, n)

            for t in range(NF):
                setup_done(t_.transpose(work[:, 0:P], down_sb[:, t, :], ident[:, :]))
            for h in range(RH):
                setup_done(t_.transpose(work[:, 0:P], wq_sb[:, h, :, :].rearrange("p a n -> p (a n)"), ident[:, :]))
                setup_done(t_.transpose(work[:, 0:NKEYS], keys_sb[:, h, :, :].rearrange("k a n -> k (a n)"), ident[0:NKEYS, 0:NKEYS]))
                for s in range(2):
                    r = slice(HALF * s, HALF * (s + 1))
                    setup_done(t_.matmul(work[:, 0:NKEYS], wqT[r, :], keysT[r, :], start=True, stop=True))

            for s in (work_filled, max_filled, scores_filled, probs_used, next_filled):
                pe.sem_inc(s, START)
            def tokens(c):
                return slice(c * CHUNK, (c + 1) * CHUNK)

            def task(p, phase, t):
                if t not in p.work:
                    return
                kind, b = t[0], p.batch(phase, t)
                pe.wait_ge(work_copied, START + p.base + p.work[t])
                if kind == "negmaxT":
                    pe.wait_ge(negmax_ready, START + b * NC + t[1] + 1)
                    for n in range(TPC):
                        ins = t_.transpose(workb[:, n * P:(n + 1) * P], negmax_pad[:, n, :], identb[:, :])
                elif kind == "sim":
                    n = t[1]
                    if phase == "M":
                        pe.wait_ge(xnT_moved, START + 16 * (b + 1))
                    ins = t_.matmul(work[:, :], xnT[:, n * P:(n + 1) * P],
                                    wsim[:, :, :, :].rearrange("p a h k -> p (a h k)"), start=True, stop=True)
                elif kind == "y":
                    k = t[1] * GROUPS + t[2]
                    pe.wait_ge(yT4_ready, START + b * NC * GROUPS + k + 1)
                    for n in range(TPC):
                        ins = t_.transpose(work[:, n * P:(n + 1) * P], yT4[:, n * P:(n + 1) * P], ident[:, :])
                elif kind == "yT":
                    for n in range(TPC):
                        ins = t_.transpose(work[:, n * P:(n + 1) * P],
                                           ytm[:, n, :, :].rearrange("p h d -> p (h d)"), ident[:, :])
                elif kind == "experts":
                    pe.wait_ge(coef_ready, START + b * NT + (t[1] + 1) * TPC)
                    for n in range(TPC):
                        ins = t_.transpose(work[:, n * P:(n + 1) * P], coef[:, n, t[2] * P:(t[2] + 1) * P],
                                           ident[:, :])
                elif kind == "out":
                    c = t[1]
                    t_.matmul(work[:, :], wproj_sb[:, :], yT[:, :], start=True, stop=False)
                    for f in range(NF):
                        t_.matmul(work[:, :], wd_sb[:, f, :], hT[:, c, f, :], start=False, stop=False)
                        ins = t_.matmul(work[:, :], up_sb[:, f, :], gT[:, c, f, :], start=False, stop=f == NF - 1)
                elif kind == "outT":
                    for n in range(TPC):
                        ins = t_.transpose(work[:, n * P:(n + 1) * P], oT[:, n * P:(n + 1) * P], ident[:, :])
                ins.then_inc(work_filled, 1)

            def ahead(b, t):
                kind, n, k = t[0], t[-1], NEXT[t]
                bank = mbank[:, k % 2, :]
                if k < 2:
                    pe.wait_ge(max_read, START + b * MUNITS)
                else:
                    before = [u for u in NEXT if NEXT[u] == k - 2][0]
                    if READER[before] == "scalar":
                        pe.wait_ge(next_read_scalar, START + b * NREAD["scalar"] + reads(before))
                    else:
                        pe.wait_ge(next_read_vector, START + b * NREAD["vector"] + reads(before))
                if kind == "xT":
                    pe.wait_ge(xn_ready, START + b * NT + (n + 1) * TPC)
                    for m in range(TPC):
                        ins = t_.transpose(bank[:, m * P:(m + 1) * P], xn[:, n * TPC + m, :], ident[:, :])
                elif kind == "qkv":
                    if n % TPC == 0:
                        pe.wait_ge(next_read_vector, START + b * NREAD["vector"] + reads(("xT", n // TPC)))
                    ins = t_.matmul(bank[:, 0:3 * D], xnT_next[:, n * P:(n + 1) * P], wqkv_sb[:, :],
                                    start=True, stop=True)
                elif kind == "parts":
                    pe.wait_ge(parts_ready, START + b * NT + n + 1)
                    for a in range(2):
                        for s in range(3):
                            m = 3 * a + s
                            ins = t_.transpose(mbankb[k % 2][:, m * P:(m + 1) * P],
                                               parts[:, n % 2, s, a * D:(a + 1) * D], identb[:, :])
                else:
                    w = {"down": downT, "gate": wg_sb, "up": wu_sb}[kind]
                    ins = t_.matmul(bank, w[:, n * P:(n + 1) * P], xnT[:, tokens(t[1])], start=True, stop=True)
                ins.then_inc(next_filled, 1)

            def side(p, phase, k):
                for t in p.side(phase, k):
                    if t in NEXT:
                        ahead(p.j, t)
                    else:
                        task(p, phase, t)

            def max_unit(i, k, unit):
                it, k0, w, heads = unit
                if k >= 2:
                    pe.wait_ge(max_read, START + i * MUNITS + k - 1)
                elif k == 0:
                    pe.wait_ge(next_read_vector, START + (i + 1) * NREAD["vector"])
                for s, h in enumerate(heads):
                    r = slice(HALF * (h % 2), HALF * (h % 2) + ROWS)
                    diag = k0 + w == P * (it + 1)
                    ins = t_.matmul(mbank[:, k % 2, s * w:(s + 1) * w], qs[r, h // 2, it * P:(it + 1) * P],
                                    ks[r, h // 2, k0:k0 + w], start=True, stop=not diag)
                    if diag:
                        ins = t_.matmul(mbank[:, k % 2, (s + 1) * w - P:(s + 1) * w], identb[:, :],
                                        mask_qk[:, :], start=False, stop=True)
                ins.then_inc(max_filled, 1)

            def scores(i, c, k, unit):
                gr, kt, u, q0 = unit
                pe.wait_ge(probs_ready, START + i * UNITS + max(k - 1, 0))
                for j in range(2):
                    r = slice(HALF * j, HALF * j + ROWS)
                    diag = kt >= c * TPC
                    ins = t_.matmul(sbank[:, k % 2, j, q0:CHUNK], ks[r, 2 * gr + u, kt * P:(kt + 1) * P],
                                    qs[r, 2 * gr + u, c * CHUNK + q0:(c + 1) * CHUNK],
                                    start=True, stop=not diag)
                    if diag:
                        ins = t_.matmul(sbank[:, k % 2, j, q0:q0 + P], identb[:, :], mask_kq[:, :],
                                        start=False, stop=True)
                ins.then_inc(scores_filled, 1)

            def values(i, c, k, unit):
                gr, kt, _, q0 = unit
                pe.wait_ge(probs_ready, START + i * UNITS + k + 2)
                if kt == 0:
                    pe.wait_ge(yT4_ready, START + i * NC * GROUPS + c * GROUPS + gr)
                last = kt == (c + 1) * TPC - 1
                for j in range(4):
                    v0 = (4 * gr + j) * (DH + 1)
                    ins = t_.matmul(ybank[32 * j:32 * j + 32, q0:CHUNK], vaug[:, kt, v0:v0 + 32],
                                    pT[:, (k + j // 2) % NPT, j % 2, q0:CHUNK], start=kt == 0, stop=last)
                ins.then_inc(probs_used, 1)

            later = max_units(1)

            def attention(p, c):
                i = p.i
                pe.wait_ge(negmax_loaded, START + (i * NC + c + 1) * 2 * 16)
                if c == 0:
                    pe.wait_ge(v_moved, START + 16 * (i + 1))
                units = exp_units(c)
                base = sum(NU[:c])
                for n, unit in enumerate(units):
                    maxima = list(pieces(NM[1], NU[0], n)) if c == 0 else []
                    for m in maxima[:1]:
                        max_unit(i, NM[0] + m, later[m])
                    scores(i, c, base + n, unit)
                    for m in maxima[1:2]:
                        max_unit(i, NM[0] + m, later[m])
                    if n >= 3 and n % 2 == 1:
                        values(i, c, base + n - 3, units[n - 3])
                    for m in maxima[2:]:
                        max_unit(i, NM[0] + m, later[m])
                    side(p, "CD"[c], n)
                values(i, c, base + NU[c] - 2, units[-2])

            def run(p):
                if p is FIRST:
                    for t in ALONE:
                        if t in NEXT:
                            ahead(p.j, t)
                else:
                    pe.wait_ge(parts_loaded, START + (p.i + 1) * (NSTACK * 16))
                    for k, unit in enumerate(max_units(0)):
                        max_unit(p.i, k, unit)
                        side(p, "B", k)
                    for c in range(NC):
                        task(p, "BC"[c], ("negmaxT", c))
                        attention(p, c)
                if p.j is not None:
                    pe.wait_ge(xnT_moved, START + 16 * (p.j + 1))
                for k, t in enumerate(mlp_tasks()):
                    if p.j is not None:
                        ahead(p.j, t)
                    side(p, "M", k)

            run(FIRST)
            with pe.Fori(0, B - 1) as i:
                run(loop_pass(i))
            run(LAST)


_INS = ['L0_attn_x', 'L0_attn_Wqkv', 'L0_attn_Wproj', 'L0_ffn_Wg', 'L0_ffn_bg', 'L0_ffn_Wu', 'L0_ffn_bu', 'L0_ffn_Wd',
        'L0_ffn_bd', 'L0_ffn_Wq', 'L0_ffn_keys', 'L0_ffn_down_embed', 'L0_ffn_up_embed']


def rope_table():
    inv = np.float32(1.0) / np.float32(10000.0) ** (np.arange(0, DH, 2, dtype=np.float32) / np.float32(DH))
    angle = np.arange(T, dtype=np.float32)[:, None] * inv[None, :].astype(np.float32)
    cos = np.repeat(np.cos(angle), 2, axis=-1)
    sin = np.repeat(np.sin(angle), 2, axis=-1) * np.tile(np.array([-1.0, 1.0], np.float32), DH // 2)
    return np.stack([cos, sin]).astype(np.float32)


def kernel(**inputs):
    import concourse.bacc as bacc
    from concourse.bass_utils import run_bass_kernel_spmd

    nc = bacc.Bacc("TRN2", target_bir_lowering=False, num_devices=1)
    arrays = {f"in_{n}": np.ascontiguousarray(inputs[n]) for n in _INS}
    arrays["rope_table"] = rope_table()
    args = [nc.dram_tensor(n, a.shape, mybir.dt.from_np(a.dtype), kind="ExternalInput").ap()
            for n, a in arrays.items()]
    out = nc.dram_tensor("out_0", (B, T, D), F32, kind="ExternalOutput").ap()
    build(nc, *args, out)
    return run_bass_kernel_spmd(nc, [arrays], core_ids=[0]).results[0]["out_0"]
```

```python
import numpy as np
import concourse.bass as bass
from concourse import mybir
from contextlib import ExitStack

F32 = mybir.dt.float32
BF16 = mybir.dt.bfloat16
ALU = mybir.AluOpType
ACT = mybir.ActivationFunctionType
AX = mybir.AxisListType

START = 1

B, T, D = 4, 1024, 128
H, DH = 16, 8
F = 512
NEXP, NKEYS, RH, KPH = 512, 64, 4, 8
HALF = D // 2
P = 128
NT = T // P
CHUNK = 512
NC = T // CHUNK
TPC = CHUNK // P
NF = F // P
PAIRS = H // 2
GROUPS = H // 4
XI = NEXP // NKEYS
TERMS = [(0, 0), (0, 1), (1, 0), (0, 2), (1, 1), (2, 0)]
KQ = len(TERMS) * DH
ROWS = P // 2
SCALE = float(DH) ** -0.5
MASKED = -1.0e30
EPS = 1e-5
NCAND = 20



def max_units(st):
    c, half = st // 2, st % 2
    units = []
    for i in range(c * TPC, (c + 1) * TPC):
        for k0 in range(0, P * (i + 1), CHUNK):
            w = min(CHUNK, P * (i + 1) - k0)
            n = max(1, CHUNK // w)
            units += [(i, k0, w, list(range(h + e, h + 2 * n, 2)))
                      for h in range(half * H // 2, (half + 1) * H // 2, 2 * n) for e in range(2)]
    return units


STAGES_A = 2 * NC
EXP_UNITS = []
for _c in range(NC):
    for _g in range(GROUPS):
        for _kt in range((_c + 1) * TPC):
            EXP_UNITS += [(len(EXP_UNITS) // 4, _g, _kt, 4 * _g + _j, max(0, _kt - _c * TPC) * P) for _j in range(4)]
UNITS = len(EXP_UNITS)
PRODS = UNITS // 4
CHUNK1 = GROUPS * TPC * 4
STAGE_STARTS = [0, CHUNK1 // 2, CHUNK1, (CHUNK1 + UNITS) // 2]
NRING = 4
NSB = 2


def chunk_of(n):
    return int(n >= CHUNK1)


def last_product(c, g):
    return (0, CHUNK1)[c] // 4 + (g + 1) * (c + 1) * TPC - 1


COPIERS = ("scalar", "vector")
COPIED_BY = {k: "scalar" for k in ("negmaxT", "sim", "down", "gate", "yT")}
COPIED_BY.update({k: "vector" for k in ("max", "xT", "qkv", "parts", "up", "experts", "y", "outT")})
SUMS = [("hidden", c, NF - 1) for c in range(NC)] + [("out", c, NF) for c in range(NC)]
NSUM = len(SUMS)
RETRIEVAL = [("sim", 0), ("top", 1.5), ("cand", 2.5), ("best", 3.5), ("dif", 4.3), ("weights", 6.5),
             ("zsum", 8), ("zinv", 9), ("keep", 11), ("inside", 16), ("clip", 17)]
STAGES = [kind for kind, _ in RETRIEVAL]
PREPARE = ("ln", "xn", "xT", "qkv", "split", "parts", "gate", "up")


EARLY = 14
PHASES = [("A", len(max_units(0)) + EARLY, 0.75), ("P", UNITS, 0.85), ("M", 2 * NC * NF, 1.35)]
MAX_BY = [0, 6, 46, 108]
RETRIEVE_AT = [("M", 9.5, 0), ("A", 7, 0), ("P", 4, 0), ("P", 24, 0), ("P", 46, 0), ("P", 68, 0), ("P", 90, 0),
               ("P", 112, 0)]
EXPERTS_AT = (43, 136)
PREP_AT, PREP_STEP = 92, 10


def build_slots():
    slots = {}
    line, now, begin = [], 0.0, {}
    for phase, steps, length in PHASES:
        begin[phase] = now
        for k in range(steps):
            line.append((now, phase, k))
            now += length
    total = now

    def put(phase, step, *tasks):
        slots.setdefault((phase, step), []).extend(tasks)

    def put_at(time, *tasks):
        time %= total
        _, phase, k = next((e for e in line if e[0] >= time), line[0])
        put(phase, k, *tasks)

    first = len(max_units(0))
    for k in range(first):
        put("A", k, ("max", 0, k))
    put("A", first, ("negate", 0))
    for k in range(EARLY):
        put("A", first + k, ("max", 1, k))
    put("A", first + 2, ("negmaxT", 0))
    for st in range(1, STAGES_A):
        todo = list(range(EARLY if st == 1 else 0, len(max_units(st))))
        k0, k1 = MAX_BY[st - 1], MAX_BY[st]
        for n, m in enumerate(todo):
            put("P", k0 + (k1 - k0) * n // len(todo), ("max", st, m))
        put("P", k1, ("negate", st))
        put("P", k1 + 3, ("negmaxT", st))
    for n, (phase, start, slack) in enumerate(RETRIEVE_AT):
        for kind, after in RETRIEVAL:
            at = begin[phase] + start + (after if after < 11 else after + slack)
            if kind == "keep":
                for h in range(RH):
                    put_at(at + 1.2 * h, (kind, n, h))
            else:
                put_at(at, (kind, n))
    for e in range(NF):
        put_at(begin["P"] + EXPERTS_AT[0] + 2.4 * e, ("experts", 0, e))
        put_at(begin["P"] + EXPERTS_AT[1] + 2.4 * e, ("experts", 1, e))
        for c in range(NC):
            put("A", 2 + 12 * c + 3 * e, ("down", c, e))
            put(*("A", 18 + 4 * e) if c == 0 else ("P", 1 + 3 * e), ("hidden", c, e))
    for c in range(NC):
        for g in range(GROUPS):
            at = 4 * (last_product(c, g) + 1) + 2
            put(*(("P", at) if at < UNITS else ("M", 0)), ("ycopy", c, g))
            put(*(("P", at + 3) if at < UNITS else ("M", 1)), ("y", c, g))
    put("P", CHUNK1 + 10, ("yT", 0))
    for e in range(NF + 1):
        put("P", CHUNK1 + 13 + 2 * e, ("out", 0, e))
        put("M", 4 + e // 3, ("out", 1, e))
    put("P", CHUNK1 + 26, ("outT", 0))
    put("M", 3, ("yT", 1))
    put("M", 8, ("outT", 1))
    put("P", PREP_AT - 20, ("ln",))
    for c in range(NC):
        put("P", PREP_AT - 12 + 4 * c, ("xn", c))
        put("P", PREP_AT - 8 + 4 * c, ("xT", c))
    for n in range(NT + 1):
        at = PREP_AT + PREP_STEP * n
        if n >= 1:
            put("P", at - 2, ("split", n - 1))
        if n < NT:
            put("P", at, ("qkv", n))
        if n >= 1:
            put("P", at + 3, ("parts", n - 1))
    for k, t in enumerate((kind, c, f) for c in range(NC) for kind in ("gate", "up") for f in range(NF)):
        slots.setdefault(("M", k), []).insert(int(k == 0), t)
    return slots


SLOTS = build_slots()
ALONE = [("ln",), ("xn", 0), ("xT", 0), ("xn", 1), ("xT", 1)]
for _n in range(NT + 1):
    if _n < NT:
        ALONE.append(("qkv", _n))
    if _n >= 1:
        ALONE += [("split", _n - 1), ("parts", _n - 1)]


def is_next(phase, t):
    return t[0] in PREPARE or phase == "M" and t[0] in STAGES


class Pass:

    def __init__(self, i, j, base=0, copy_base=None):
        self.i, self.j = i, j
        self.base = base
        self.copy_base = copy_base or {r: 0 for r in COPIERS}
        self.steps = [("P", 0, ALONE)] if i is None else []
        for phase, count, _ in PHASES:
            if i is not None or phase == "M":
                self.steps += [(phase, k, [t for t in SLOTS.get((phase, k), [])
                                           if (j if is_next(phase, t) else i) is not None]) for k in range(count)]
        self.order = [t for _, _, tasks in self.steps for t in tasks if t[0] in COPIED_BY]
        self.ring = {t: k for k, t in enumerate(self.order)}
        self.count = {r: sum(COPIED_BY[t[0]] == r for t in self.order) for r in COPIERS}
        self.nth = {t: sum(COPIED_BY[u[0]] == COPIED_BY[t[0]] for u in self.order[:k + 1])
                      for k, t in enumerate(self.order)}

    def batch(self, phase, t):
        return self.j if is_next(phase, t) else self.i


FIRST = Pass(None, 0)
FULL = Pass(0, 1)


def bases(i):
    return len(FIRST.order) + i * len(FULL.order), {r: FIRST.count[r] + i * FULL.count[r] for r in COPIERS}


def loop_pass(i):
    return Pass(i, i + 1, *bases(i))


LAST = Pass(B - 1, None, *bases(B - 1))


class Steps:

    def __init__(self, engine, sem, per_pass):
        self.engine, self.sem, self.per, self.base, self.n, self.first = engine, sem, per_pass, 0, 0, 0

    def begin(self, p):
        if p.i is not None:
            self.first = self.first or self.n
            self.base = self.first + p.i * self.per
        self.n = 0

    def mark(self, ins):
        ins.then_inc(self.sem, 1)
        self.n += 1
        return self.n

    def need(self, n):
        self.engine.wait_ge(self.sem, START + self.base + n)

    def end(self, p):
        if p.i is not None:
            assert self.n == (self.per if p.j is not None else self.per - self.first), (self.n, self.per, self.first)


def build(nc, x, wqkv, wproj, wg, bg, wu, bu, wd, bd, wq, keys, down, up, rope, out):
    ctx = ExitStack()
    with ctx:
        def sb(name, shape, dt=F32):
            return ctx.enter_context(nc.sbuf_tensor(name, shape, dt))

        def sem(name):
            return ctx.enter_context(nc.semaphore(name))

        parts_dram = nc.dram_tensor("parts_scratch", (2, 3, P, T), BF16, kind="Internal").ap()
        negmax_dram = nc.dram_tensor("negmax_scratch", (2, 2, 3, PAIRS // 2, T), BF16, kind="Internal").ap()

        ident = sb("ident", [P, P])
        identb = sb("identb", [P, P], BF16)
        mask_qk = sb("mask_qk", [P, P], BF16)
        mask_kq = sb("mask_kq", [P, P], BF16)
        rope_sb = sb("rope_sb", [P, 2, NT, DH])
        wqkv_sb = sb("wqkv_sb", [P, 3 * D])
        wproj_sb = sb("wproj_sb", [P, D])
        wg_sb = sb("wg_sb", [P, F])
        wu_sb = sb("wu_sb", [P, F])
        wd_sb = sb("wd_sb", [P, NF, D])
        up_sb = sb("up_sb", [P, NF, D])
        downT = sb("downT", [P, NEXP])
        wsim = sb("wsim", [P, 2, RH, NKEYS])
        bg_sb = sb("bg_sb", [P, NF])
        bu_sb = sb("bu_sb", [P, NF])
        bd_sb = sb("bd_sb", [P, 1])
        half_neg = sb("half_neg", [P, NT])
        eps = sb("eps", [P, NT])
        NPAD = ROWS - KQ
        pad_rows = sb("pad_rows", [NPAD, 2, T], BF16)
        zero_rows = pad_rows[0:3, 0:1, :]
        carrier = sb("carrier", [P, 1])
        NPT = 3
        pT = sb("pT", [P, NPT, 4, CHUNK])
        wq_sb = pT[:, 0, 0, :].rearrange("p (h a n) -> p h a n", h=RH, a=2)
        keys_sb = pT[0:NKEYS, 0, 1, :].rearrange("p (h a n) -> p h a n", h=RH, a=2)
        down_sb = pT[:, 0, 2, :].rearrange("p (t d) -> p t d", t=NF)
        wqT = sb("wqT", [P, P])
        keysT = sb("keysT", [P, NKEYS])

        xin = sb("xin", [P, NT, D])
        stats = sb("stats", [P, NT, 6])
        meanvar = sb("meanvar", [P, NT, 2])
        vareps = sb("vareps", [P, NT])
        rstd = sb("rstd", [P, NT])
        xn = sb("xn", [P, NT, D])
        xnT_next = sb("xnT_next", [P, T])
        xnT = sb("xnT", [P, T])
        qk = sb("qk", [P, 2, 2 * H, DH])
        rot_a = sb("rot_a", [P, 2, 2 * H, DH])
        rot_b = sb("rot_b", [P, 2, 2 * H, DH])
        rot = sb("rot", [P, 2 * H, DH])
        rest = sb("rest", [P, 2 * D])
        parts = sb("parts", [P, 2, 3, 2 * D], BF16)
        partsT = sb("partsT", [P, 2, 3, T], BF16)
        qs = sb("qs", [P, PAIRS, T], BF16)
        ks = sb("ks", [P, PAIRS, T], BF16)
        VW = (H - 1) * (DH + 1) + 32
        vaug = sb("vaug", [P, NT, VW])
        vaug_next = sb("vaug_next", [P, NT, VW])
        vheads = vaug_next[:, :, 0:H * (DH + 1)].rearrange("p n (h d) -> p n h d", d=DH + 1)

        pmax = sb("pmax", [P, NT, 2, H])
        rmax = sb("rmax", [P, TPC, H // 2])
        mrest = sb("mrest", [P, TPC, H // 2])
        negmax_pad = sb("negmax_pad", [P, TPC, P], BF16)
        negmax = negmax_pad[:, :, 0:3 * H // 2].rearrange("p n (e s j) -> p n e s j", e=2, s=3)
        negmaxT = sb("negmaxT", [3 * H // 2, CHUNK], BF16)
        yT4 = sb("yT4", [P, CHUNK])
        ytm = sb("ytm", [P, TPC, H, DH])
        yinv = sb("yinv", [P, TPC, 4])
        yT = sb("yT", [P, CHUNK])

        sgate = sb("sgate", [P, NC, NF, CHUNK])
        hT = sgate
        sexp = sb("sexp", [P, NC, NF, CHUNK])
        gT = sexp
        sim = sb("sim", [P, 2 * RH, NKEYS])
        simx = sb("simx", [P, RH, XI])
        top = sb("top", [P, 2 * RH, KPH])
        cand = sb("cand", [P, RH, NCAND])
        best = sb("best", [P, RH, KPH])
        ND = RH * (KPH + XI + NKEYS)
        dif = sb("dif", [P, ND])
        edif = sb("edif", [P, ND])
        zsum = sb("zsum", [P, RH])
        zinv = sb("zinv", [P, RH])
        exz = sb("exz", [P, RH, XI])
        ssum = sb("ssum", [P, RH, XI, NKEYS])
        wsum = sb("wsum", [P, RH, XI * NKEYS])
        coef4 = wsum
        inside = sb("inside", [P, RH])
        inside1 = sb("inside1", [P, 1])
        clipped = sb("clipped", [P, 1])
        coef = sb("coef", [P, TPC, NEXP])
        hidden_sum = sb("hidden_sum", [P, NC, CHUNK])
        oT = sb("oT", [P, CHUNK])
        xres = sb("xres", [P, TPC, D])
        osb = sb("osb", [P, TPC, D])

        sum_bank = ctx.enter_context(nc.psum_tensor("sum_bank", [P, CHUNK], F32))
        ring = ctx.enter_context(nc.psum_tensor("ring", [P, NRING, CHUNK], F32))
        sbank = ctx.enter_context(nc.psum_tensor("sbank", [P, NSB, CHUNK], F32))
        ybank = ctx.enter_context(nc.psum_tensor("ybank", [P, CHUNK], F32))
        ringb = [ring[:, k, :].bitcast(BF16) for k in range(NRING)]

        weights_loaded = sem("weights_loaded")
        consts_made = sem("consts_made")
        pool_setup = sem("pool_setup")
        pads_stored = sem("pads_stored")
        setup_filled = sem("setup_filled")
        setup_copied = sem("setup_copied")
        x_loaded = sem("x_loaded")
        res_loaded = sem("res_loaded")
        stats_done = sem("stats_done")
        var_ready = sem("var_ready")
        rstd_ready = sem("rstd_ready")
        xn_ready = sem("xn_ready")
        ring_filled = sem("ring_filled")
        ring_copied_scalar = sem("ring_copied_scalar")
        ring_copied_vector = sem("ring_copied_vector")
        ring_copied = {"scalar": ring_copied_scalar, "vector": ring_copied_vector}
        sum_filled = sem("sum_filled")
        sum_read = sem("sum_read")
        qk_copied = sem("qk_copied")
        rot_ready = sem("rot_ready")
        parts_ready = sem("parts_ready")
        parts_stored = sem("parts_stored")
        parts_loaded = sem("parts_loaded")
        xnT_moved = sem("xnT_moved")
        v_moved = sem("v_moved")
        negmax_ready = sem("negmax_ready")
        negmax_stored = sem("negmax_stored")
        negmax_loaded = sem("negmax_loaded")
        scores_filled = sem("scores_filled")
        probs_ready = sem("probs_ready")
        probs_used = sem("probs_used")
        yT4_ready = sem("yT4_ready")
        dif_ready = sem("dif_ready")
        edif_ready = sem("edif_ready")
        zinv_ready = sem("zinv_ready")
        pairs_ready = sem("pairs_ready")
        weighed = sem("weighed")
        clipped_ready = sem("clipped_ready")
        kept_ready = sem("kept_ready")
        coef_ready = sem("coef_ready")
        out_stored = sem("out_stored")
        pool_steps = sem("pool_steps")
        dve_steps = sem("dve_steps")

        block = ctx.enter_context(nc.Block())
        x_v = x.rearrange("b (n p) d -> b p n d", p=P)
        o_v = out.rearrange("b (n p) d -> b p n d", p=P)
        NLOAD = 15
        NCONST = 11
        NSTACK = (len(TERMS) * 2 + 1) * 2

        SETUP = [downT[:, t * P:(t + 1) * P] for t in range(NF)]
        for h in range(RH):
            SETUP += [wqT[:, :], keysT[:, :], wsim[:, 0, h, :], wsim[:, 1, h, :]]

        def filled(e, p, t):
            e.wait_ge(ring_filled, START + p.base + p.ring[t] + 1)

        def filled_before(e, p, t=None):
            e.wait_ge(ring_filled, START + p.base + (p.ring[t] + 1 if t else 0))

        def copied(e, p, t):
            e.wait_ge(ring_copied[COPIED_BY[t[0]]], START + p.copy_base[COPIED_BY[t[0]]] + p.nth[t])

        def bank_of(p, t):
            return ring[:, p.ring[t] % NRING, :]

        @block.sync
        def _(sp):
            for s in (x_loaded, res_loaded, parts_stored, parts_loaded, negmax_stored, negmax_loaded,
                      out_stored, xnT_moved, v_moved):
                sp.sem_inc(s, START)
            sp.dma_start(xin[:, :, :], x_v[0]).then_inc(x_loaded, 16)
            for dst, src in [
                (wqkv_sb[:, :], wqkv), (wproj_sb[:, :], wproj), (wg_sb[:, :], wg), (wu_sb[:, :], wu),
                (wd_sb[:, :, :], wd.rearrange("(t p) c -> p t c", p=P)),
                (up_sb[:, :, :], up.rearrange("(t p) c -> p t c", p=P)),
                (down_sb[:, :, :], down.rearrange("(t p) c -> p t c", p=P)),
                (wq_sb[:, :, 0, :], wq[:, 0:RH * HALF].rearrange("d (h n) -> d h n", h=RH)),
                (wq_sb[:, :, 1, :], wq[:, RH * HALF:].rearrange("d (h n) -> d h n", h=RH)),
                (keys_sb[:, :, :, :], keys.rearrange("h k a n -> k h a n")),
                (bg_sb[:, :], bg.rearrange("(t p) -> p t", p=P)),
                (bu_sb[:, :], bu.rearrange("(t p) -> p t", p=P)),
                (bd_sb[:, :], bd.rearrange("(p a) -> p a", a=1)),
                (rope_sb[:, 0, :, :], rope[0].rearrange("(n p) d -> p n d", p=P)),
                (rope_sb[:, 1, :, :], rope[1].rearrange("(n p) d -> p n d", p=P)),
            ]:
                sp.dma_start(dst, src, allow_slow_non_contiguous=True).then_inc(weights_loaded, 16)

            sp.wait_ge(consts_made, NCONST)
            for k, dst in ((0, qs), (1, ks)):
                for hh in range(2):
                    r = HALF * hh + KQ
                    sp.dma_start(dst[r:r + NPAD, :, :], pad_rows[:, k:k + 1, :].to_broadcast([NPAD, PAIRS, T]))\
                        .then_inc(pads_stored, 16)
            sp.wait_ge(pads_stored, 16 * 4)

            def load_rows(dst, batch, n0, n1, loaded):
                sp.dma_start(dst, batch[:, :, n0:n1, :].rearrange("b p n d -> (b p) n d")).then_inc(loaded, 16)

            def run(p, rows, next_rows, out_rows):
                i, j = p.i, p.j
                if i is not None and j is not None:
                    sp.wait_ge(xn_ready, START + j * NT)
                    load_rows(xin[:, :, :], next_rows, 0, NT, x_loaded)
                if i is not None:
                    sp.wait_ge(ring_copied_vector, START + p.copy_base["vector"])
                    load_rows(xres[:, :, :], rows, 0, TPC, res_loaded)
                    for st in range(STAGES_A):
                        c, half = st // 2, st % 2
                        cols = slice(c * CHUNK, (c + 1) * CHUNK)
                        if st == STAGES_A - 1:
                            copied(sp, p, ("outT", 0))
                            sp.dma_start(out_rows[:, :, 0:TPC, :].rearrange("b p n d -> (b p) n d"), osb[:, :, :])\
                                .then_inc(out_stored, 16)
                            load_rows(xres[:, :, :], rows, TPC, NT, res_loaded)
                        copied(sp, p, ("negmaxT", st))
                        sp.dma_start(negmax_dram[half].rearrange("h s j t -> (h s j) t")[:, cols], negmaxT[:, :])\
                            .then_inc(negmax_stored, 16)
                        sp.wait_ge(negmax_stored, START + (i * STAGES_A + st + 1) * 16)
                        for hh in range(2):
                            r = HALF * hh + KQ
                            sp.dma_start(qs[r:r + 3, half * PAIRS // 2:(half + 1) * PAIRS // 2, cols],
                                         negmax_dram[half, hh][:, :, cols]).then_inc(negmax_loaded, 16)
                if j is not None:
                    filled(sp, p, ("qkv", NT - 1))
                    sp.dma_start(xnT[:, :], xnT_next[:, :]).then_inc(xnT_moved, 16)
                    copied(sp, p, ("parts", NT - 1))
                    for s in range(3):
                        for a in range(2):
                            sp.dma_start(parts_dram[a, s], partsT[:, a, s, :]).then_inc(parts_stored, 16)
                    sp.wait_ge(scores_filled, START + j * UNITS)
                    for hh in range(2):
                        r = HALF * hh + KQ
                        sp.dma_start(qs[r:r + 3, :, :], zero_rows[:, :, :].to_broadcast([3, PAIRS, T]))\
                            .then_inc(parts_loaded, 16)
                    sp.wait_ge(parts_stored, START + (j + 1) * (6 * 16))
                    for t, pair in enumerate(TERMS):
                        for a, dst in ((0, qs), (1, ks)):
                            for hh in range(2):
                                src = parts_dram[a, pair[a]].rearrange("(j h d) t -> h d j t", h=2, d=DH)[hh]
                                r = HALF * hh + DH * t
                                sp.dma_start(dst[r:r + DH, :, :], src).then_inc(parts_loaded, 16)
                    sp.wait_ge(probs_used, START + j * PRODS)
                    sp.dma_start(vaug[:, :, :], vaug_next[:, :, :]).then_inc(v_moved, 16)
                if i is not None:
                    copied(sp, p, ("outT", 1))
                    sp.dma_start(out_rows[:, :, TPC:NT, :].rearrange("b p n d -> (b p) n d"), osb[:, :, :])\
                        .then_inc(out_stored, 16)

            run(FIRST, None, x_v[0:1], None)
            with sp.Fori(0, B - 1) as i:
                run(loop_pass(i), x_v[bass.ds(i, 1)], x_v[bass.ds(i + 1, 1)], o_v[bass.ds(i, 1)])
            run(LAST, x_v[B - 1:B], None, o_v[B - 1:B])
            sp.wait_ge(out_stored, START + B * NC * 16)

        @block.gpsimd
        def _(pool):
            g = nc.gpsimd
            for m in (ident, identb, mask_qk, mask_kq):
                g.memset(m[:, :], 0.0).then_inc(pool_setup, 1)
            pool.wait_ge(pool_setup, 4)
            for m in (ident, identb):
                g.affine_select(out=m[:, :], in_=m[:, :], pattern=[[-1, P]], compare_op=ALU.not_equal, fill=1.0,
                                base=0, channel_multiplier=1).then_inc(consts_made, 1)
            g.affine_select(out=mask_qk[:, :], in_=mask_qk[:, :], pattern=[[-1, P]], compare_op=ALU.is_ge,
                            fill=MASKED, base=0, channel_multiplier=1).then_inc(consts_made, 1)
            g.affine_select(out=mask_kq[:, :], in_=mask_kq[:, :], pattern=[[1, P]], compare_op=ALU.is_ge,
                            fill=MASKED, base=0, channel_multiplier=-1).then_inc(consts_made, 1)
            g.memset(half_neg[:, :], -0.5).then_inc(consts_made, 1)
            g.memset(eps[:, :], EPS).then_inc(consts_made, 1)
            g.memset(negmax_pad[:, :, :], 0.0).then_inc(consts_made, 1)
            for k in range(2):
                g.memset(pad_rows[:, k, :], float(k)).then_inc(consts_made, 1)
            g.memset(vaug_next[:, :, H * (DH + 1):VW], 0.0).then_inc(consts_made, 1)
            g.memset(vheads[:, :, :, DH:DH + 1], 1.0).then_inc(consts_made, 1)
            pool.wait_ge(consts_made, NCONST)
            for s in (var_ready, rstd_ready, rot_ready, pairs_ready, weighed, coef_ready, pool_steps):
                pool.sem_inc(s, START)
            steps = Steps(pool, pool_steps, 3 * NT)

            def task(p, phase, t):
                kind, n, b = t[0], t[-1] if len(t) == 2 else 0, p.batch(phase, t)
                if kind == "ln":
                    pool.wait_ge(stats_done, START + (b + 1) * NT)
                    pool.wait_ge(xn_ready, START + b * NT)
                    g.tensor_tensor(vareps[:, :], meanvar[:, :, 1], eps[:, :], ALU.add).then_inc(var_ready, 1)
                    pool.wait_ge(var_ready, START + b + 1)
                    g.tensor_tensor(rstd[:, :], vareps[:, :], half_neg[:, :], ALU.pow).then_inc(rstd_ready, 1)
                elif kind == "qkv":
                    if p is FIRST and n == 0:
                        pool.wait_ge(weights_loaded, 16 * NLOAD)
                    pool.wait_ge(qk_copied, START + b * NT + n + 1)
                    pool.wait_ge(parts_ready, START + b * NT + max(n - 1, 0))
                    sin = rope_sb[:, 1, n:n + 1, :].rearrange("p o (e t) -> p o e t", t=2)
                    a2 = qk[:, n % 2, :, :].rearrange("p h (e t) -> p h e t", t=2)
                    b2 = rot_b[:, n % 2, :, :].rearrange("p h (e t) -> p h e t", t=2)
                    for e in range(2):
                        g.tensor_tensor(b2[:, :, :, e], a2[:, :, :, 1 - e],
                                        sin[:, :, :, e].to_broadcast([P, 2 * H, DH // 2]), ALU.mult)\
                            .then_inc(rot_ready, 1)
                elif kind == "sim":
                    copied(pool, p, ("sim", n))
                    pool.wait_ge(kept_ready, START + (b * NT + n) * RH)
                    for h in range(RH):
                        g.tensor_tensor(ssum[:, h, :, :],
                                        sim[:, h, 0:XI].unsqueeze(2).to_broadcast([P, XI, NKEYS]),
                                        sim[:, RH + h:RH + h + 1, :].to_broadcast([P, XI, NKEYS]), ALU.add)\
                            .then_inc(pairs_ready, 1)
                elif kind == "zinv":
                    pool.wait_ge(zinv_ready, START + b * NT + n + 1)
                    k = steps.mark(g.tensor_tensor(
                        exz[:, :, :], edif[:, RH * KPH:RH * (KPH + XI)].rearrange("p (h i) -> p h i", h=RH),
                        zinv[:, :].unsqueeze(2).to_broadcast([P, RH, XI]), ALU.mult))
                    steps.need(k)
                    ey = edif[:, RH * (KPH + XI):].rearrange("p (h j) -> p h j", h=RH)
                    for h in range(RH):
                        g.tensor_tensor(wsum[:, h, :].rearrange("p (i j) -> p i j", i=XI),
                                        exz[:, h, :].unsqueeze(2).to_broadcast([P, XI, NKEYS]),
                                        ey[:, h:h + 1, :].to_broadcast([P, XI, NKEYS]), ALU.mult)\
                            .then_inc(weighed, 1)
                elif kind == "clip":
                    pool.wait_ge(kept_ready, START + (b * NT + n + 1) * RH)
                    k = steps.mark(g.tensor_tensor(coef4[:, 0:2, :], coef4[:, 0:2, :], coef4[:, 2:4, :], ALU.add))
                    steps.need(k)
                    filled_before(pool, p, ("experts", n // TPC - 1, NF - 1) if n >= TPC else None)
                    c = n % TPC
                    pool.wait_ge(clipped_ready, START + b * NT + n + 1)
                    k = steps.mark(g.tensor_tensor(coef[:, c, :], coef4[:, 0, :], coef4[:, 1, :], ALU.add))
                    steps.need(k)
                    g.tensor_tensor(coef[:, c, NEXP - 1:NEXP], coef[:, c, NEXP - 1:NEXP], clipped[:, :], ALU.add)\
                        .then_inc(coef_ready, 1)
                    pool.wait_ge(coef_ready, START + b * NT + n + 1)

            def run(p):
                steps.begin(p)
                for phase, k, tasks in p.steps:
                    for t in tasks:
                        task(p, phase, t)
                steps.end(p)

            run(FIRST)
            with pool.Fori(0, B - 1) as i:
                run(loop_pass(i))
            run(LAST)

        @block.scalar
        def _(act):
            a = nc.scalar
            for s in (yT4_ready, edif_ready, probs_ready, ring_copied_scalar, sum_read):
                act.sem_inc(s, START)
            for n, dst in enumerate(SETUP):
                act.wait_ge(setup_filled, n + 1)
                a.activation(dst, sum_bank[:, 0:dst.shape[-1]], ACT.Copy).then_inc(setup_copied, 1)
            act.wait_ge(weights_loaded, 16 * NLOAD)
            act.wait_ge(consts_made, NCONST)
            def task(p, phase, t):
                kind, b = t[0], p.batch(phase, t)
                if t in p.ring and COPIED_BY[kind] == "scalar":
                    filled(act, p, t)
                    bank = bank_of(p, t)
                if kind == "negmaxT":
                    act.wait_ge(negmax_stored, START + (b * STAGES_A + t[1]) * 16)
                    a.activation(negmaxT[:, :], ringb[p.ring[t] % NRING][0:3 * H // 2, 0:CHUNK], ACT.Copy)\
                        .then_inc(ring_copied_scalar, 1)
                elif kind == "sim":
                    n = t[1]
                    act.wait_ge(dif_ready, START + b * NT + n)
                    act.wait_ge(pairs_ready, START + (b * NT + n) * RH)
                    a.activation(sim[:, :, :], bank.rearrange("p (g k) -> p g k", k=NKEYS), ACT.Copy)\
                        .then_inc(ring_copied_scalar, 1)
                elif kind == "weights":
                    n = t[1]
                    act.wait_ge(dif_ready, START + b * NT + n + 1)
                    act.wait_ge(weighed, START + (b * NT + n) * RH)
                    a.activation(edif[:, :], dif[:, :], ACT.Exp).then_inc(edif_ready, 1)
                elif kind == "ycopy":
                    k = t[1] * GROUPS + t[2]
                    act.wait_ge(probs_used, START + b * PRODS + last_product(t[1], t[2]) + 1)
                    filled_before(act, p, ("y", (k - 1) // GROUPS, (k - 1) % GROUPS) if k else None)
                    a.activation(yT4[:, :], ybank[:, :], ACT.Copy).then_inc(yT4_ready, 1)
                elif kind == "down":
                    a.activation(sexp[:, t[1], t[2], :], bank, ACT.Silu).then_inc(ring_copied_scalar, 1)
                elif kind == "gate":
                    _, c, f = t
                    if p.i is not None:
                        act.wait_ge(sum_filled, START + p.i * NSUM + SUMS.index(("out", c, NF)) + 1)
                    a.activation(sgate[:, c, f, :], bank, ACT.Silu, bias=bg_sb[:, f:f + 1])\
                        .then_inc(ring_copied_scalar, 1)
                elif kind == "yT":
                    a.activation(yT[:, :], bank, ACT.Copy).then_inc(ring_copied_scalar, 1)
                elif t in SUMS and kind == "hidden":
                    act.wait_ge(sum_filled, START + b * NSUM + SUMS.index(t) + 1)
                    a.activation(hidden_sum[:, t[1], :], sum_bank[:, :], ACT.Identity, bias=bd_sb[:, 0:1])\
                        .then_inc(sum_read, 1)

            def exponentials(p, n):
                prod, gr, kt, h, q0 = EXP_UNITS[n]
                act.wait_ge(scores_filled, START + p.i * UNITS + n + 1)
                act.wait_ge(probs_used, START + p.i * PRODS + max(prod + 1 - NPT, 0))
                a.activation(pT[:, prod % NPT, h % 4, q0:CHUNK], sbank[:, n % NSB, q0:CHUNK], ACT.Exp,
                             scale=SCALE).then_inc(probs_ready, 1)

            def run(p):
                for phase, k, tasks in p.steps:
                    if phase == "P" and p.i is not None:
                        exponentials(p, k)
                    for t in tasks:
                        task(p, phase, t)

            run(FIRST)
            with act.Fori(0, B - 1) as i:
                run(loop_pass(i))
            run(LAST)

        @block.vector
        def _(dve):
            v = nc.vector
            TOP_STEPS = 1 + 2 * RH + 4 + 2 + RH + 2
            steps = Steps(dve, dve_steps, NT + 5 * NT + 2 * (1 + 3) + 2 * (2 + 3) + NT * TOP_STEPS + NC * GROUPS)
            for s in (stats_done, xn_ready, qk_copied, parts_ready, negmax_ready, dif_ready, zinv_ready,
                      kept_ready, clipped_ready, ring_copied_vector, dve_steps):
                dve.sem_inc(s, START)

            def choose(p, phase, t):
                kind, n, b = t[0], t[1], p.batch(phase, t)
                xs, ys = top[:, 0:RH, :], top[:, RH:2 * RH, :]

                def wide(ap, w):
                    return ap.to_broadcast([P, RH, w])

                if kind == "top":
                    copied(dve, p, ("sim", n))
                    dve.wait_ge(kept_ready, START + (b * NT + n) * RH)
                    steps.mark(v.tensor_copy(simx[:, :, :], sim[:, 0:RH, 0:XI]))
                    for a in range(2 * RH):
                        steps.mark(v.max(top[:, a, :], sim[:, a, :]))
                elif kind == "cand":
                    steps.need(steps.n)
                    steps.mark(v.tensor_tensor(cand[:, :, 0:8], ys, wide(xs[:, :, 0:1], 8), ALU.add))
                    steps.mark(v.tensor_tensor(cand[:, :, 8:12], ys[:, :, 0:4], wide(xs[:, :, 1:2], 4), ALU.add))
                    steps.mark(v.tensor_tensor(cand[:, :, 12:16].rearrange("p h (a b) -> p h a b", a=2),
                                               ys[:, :, 0:2].unsqueeze(2).to_broadcast([P, RH, 2, 2]),
                                               xs[:, :, 2:4].unsqueeze(3).to_broadcast([P, RH, 2, 2]), ALU.add))
                    steps.mark(v.tensor_tensor(cand[:, :, 16:20], xs[:, :, 4:8], wide(ys[:, :, 0:1], 4), ALU.add))
                elif kind == "best":
                    dve.wait_ge(edif_ready, START + b * NT + n)
                    steps.need(steps.n)
                    o = RH * KPH
                    steps.mark(v.tensor_tensor(dif[:, o:o + RH * XI].rearrange("p (h i) -> p h i", h=RH),
                                               simx[:, :, :], wide(xs[:, :, 0:1], XI), ALU.subtract))
                    o += RH * XI
                    steps.mark(v.tensor_tensor(dif[:, o:].rearrange("p (h j) -> p h j", h=RH),
                                               sim[:, RH:2 * RH, :], wide(ys[:, :, 0:1], NKEYS), ALU.subtract))
                    for h in range(RH):
                        steps.mark(v.max(best[:, h, :], cand[:, h, :]))
                elif kind == "dif":
                    steps.need(steps.n)
                    v.tensor_tensor(dif[:, 0:RH * KPH].rearrange("p (h r) -> p h r", h=RH), best[:, :, :],
                                    wide(best[:, :, 0:1], KPH), ALU.subtract).then_inc(dif_ready, 1)
                elif kind == "zsum":
                    dve.wait_ge(edif_ready, START + b * NT + n + 1)
                    steps.mark(v.tensor_reduce(zsum[:, :],
                                               edif[:, 0:RH * KPH].rearrange("p (h r) -> p h r", h=RH),
                                               axis=AX.X, op=ALU.add))
                elif kind == "zinv":
                    steps.need(steps.n)
                    dve.wait_ge(weighed, START + (b * NT + n) * RH)
                    v.reciprocal(zinv[:, :], zsum[:, :]).then_inc(zinv_ready, 1)
                elif kind == "keep":
                    h = t[2]
                    dve.wait_ge(coef_ready, START + b * NT + n)
                    dve.wait_ge(weighed, START + (b * NT + n) * RH + h + 1)
                    v.scalar_tensor_tensor(out=coef4[:, h, :], in0=ssum[:, h, :, :].rearrange("p i j -> p (i j)"),
                                           scalar=best[:, h, KPH - 1:KPH], in1=wsum[:, h, :],
                                           op0=ALU.is_ge, op1=ALU.mult, accum_out=inside[:, h:h + 1])\
                        .then_inc(kept_ready, 1)
                elif kind == "inside":
                    dve.wait_ge(kept_ready, START + (b * NT + n + 1) * RH)
                    steps.mark(v.tensor_reduce(inside1[:, :], inside[:, :], axis=AX.X, op=ALU.add))
                elif kind == "clip":
                    steps.need(steps.n)
                    v.tensor_scalar(clipped[:, :], inside1[:, :], -1.0, float(RH), ALU.mult, ALU.add)\
                        .then_inc(clipped_ready, 1)

            def prepare(p, b, t):
                kind, n = t[0], t[-1]
                if kind == "ln":
                    dve.wait_ge(x_loaded, START + 16 * (b + 1))
                    for n in range(NT):
                        k = steps.mark(v.bn_stats(stats[:, n, :], xin[:, n, :]))
                    steps.need(k)
                    v.memset(carrier[:, :], 0.0)
                    for n in range(NT):
                        v.bn_aggr(meanvar[:, n, :], stats[:, n, :]).then_inc(stats_done, 1)
                elif kind == "xn":
                    dve.wait_ge(stats_done, START + (b + 1) * NT)
                    dve.wait_ge(rstd_ready, START + b + 1)
                    filled_before(dve, p)
                    for m in range(n * TPC, (n + 1) * TPC):
                        v.tensor_scalar(xn[:, m, :], xin[:, m, :], meanvar[:, m, 0:1], rstd[:, m:m + 1],
                                        ALU.subtract, ALU.mult).then_inc(xn_ready, 1)
                elif kind == "xT":
                    dve.wait_ge(xnT_moved, START + 16 * b)
                    filled(dve, p, t)
                    v.tensor_copy(xnT_next[:, n * CHUNK:(n + 1) * CHUNK], bank_of(p, t))\
                        .then_inc(ring_copied_vector, 1)
                elif kind == "qkv":
                    if p is FIRST and n == 0:
                        dve.wait_ge(weights_loaded, 16 * NLOAD)
                    filled(dve, p, t)
                    dve.wait_ge(rot_ready, START + 2 * (b * NT + max(n - 1, 0)))
                    src = bank_of(p, t)
                    v.tensor_copy(qk[:, n % 2, :, :], src[:, 0:2 * D].rearrange("p (h d) -> p h d", d=DH))\
                        .then_inc(qk_copied, 1)
                    steps.mark(v.tensor_tensor(rot_a[:, n % 2, :, :],
                                               src[:, 0:2 * D].rearrange("p (h d) -> p h d", d=DH),
                                               rope_sb[:, 0, n:n + 1, :].to_broadcast([P, 2 * H, DH]), ALU.mult))
                    dve.wait_ge(v_moved, START + 16 * b)
                    v.tensor_copy(vheads[:, n, :, 0:DH], src[:, 2 * D:3 * D].rearrange("p (h d) -> p h d", d=DH))\
                        .then_inc(ring_copied_vector, 1)
                elif kind == "split":
                    dve.wait_ge(rot_ready, START + 2 * (b * NT + n + 1))
                    steps.need(steps.n)
                    k = steps.mark(v.tensor_tensor(rot[:, :, :], rot_a[:, n % 2, :, :], rot_b[:, n % 2, :, :],
                                                   ALU.add))
                    if n >= 2:
                        filled(dve, p, ("parts", n - 2))
                    steps.need(k)
                    r = rot[:, :, :].rearrange("p h d -> p (h d)")
                    pt = parts[:, n % 2, :, :]
                    k = steps.mark(v.tensor_copy(pt[:, 0, :], r))
                    steps.need(k)
                    k = steps.mark(v.tensor_tensor(rest[:, :], r, pt[:, 0, :], ALU.subtract))
                    steps.need(k)
                    k = steps.mark(v.tensor_copy(pt[:, 1, :], rest[:, :]))
                    steps.need(k)
                    v.tensor_tensor(pt[:, 2, :], rest[:, :], pt[:, 1, :], ALU.subtract).then_inc(parts_ready, 1)
                    dve.wait_ge(parts_ready, START + b * NT + n + 1)
                elif kind == "parts":
                    dve.wait_ge(parts_stored, START + b * (6 * 16))
                    filled(dve, p, t)
                    v.tensor_copy(partsT[:, :, :, n * P:(n + 1) * P].rearrange("p a s t -> p (a s) t"),
                                  ringb[p.ring[t] % NRING][:, 0:6 * P].rearrange("p (a t) -> p a t", t=P))\
                        .then_inc(ring_copied_vector, 1)

            def task(p, phase, t):
                kind, b = t[0], p.batch(phase, t)
                if kind in PREPARE:
                    prepare(p, b, t)
                if kind in STAGES:
                    choose(p, phase, t)
                if kind in ("experts", "y", "outT", "up", "max"):
                    filled(dve, p, t)
                    bank = bank_of(p, t)
                if kind == "experts":
                    copied(dve, p, ("down", t[1], t[2]))
                    v.tensor_tensor(gT[:, t[1], t[2], :], bank, sexp[:, t[1], t[2], :], ALU.mult)\
                        .then_inc(ring_copied_vector, 1)
                elif kind == "y":
                    gr = t[2]
                    wv = bank.rearrange("p (n j d) -> p n j d", n=TPC, j=4)
                    before = t[1] * GROUPS + gr - 1
                    if before >= 0:
                        copied(dve, p, ("y", before // GROUPS, before % GROUPS))
                    k = steps.mark(v.reciprocal(yinv[:, :, :], wv[:, :, :, DH]))
                    steps.need(k)
                    v.tensor_tensor(ytm[:, :, 4 * gr:4 * gr + 4, :], wv[:, :, :, 0:DH],
                                    yinv[:, :, :].unsqueeze(3).to_broadcast([P, TPC, 4, DH]), ALU.mult)\
                        .then_inc(ring_copied_vector, 1)
                elif kind == "outT":
                    c = t[1]
                    dve.wait_ge(res_loaded, START + 16 * (b * NC + c + 1))
                    dve.wait_ge(out_stored, START + 16 * (b * NC + c))
                    v.tensor_tensor(osb[:, :, :], bank.rearrange("p (n d) -> p n d", d=D), xres[:, :, :],
                                    ALU.add).then_inc(ring_copied_vector, 1)
                elif t in SUMS and kind == "out":
                    dve.wait_ge(sum_filled, START + b * NSUM + SUMS.index(t) + 1)
                    v.tensor_tensor(oT[:, :], sum_bank[:, :], hidden_sum[:, t[1], :], ALU.add).then_inc(sum_read, 1)
                elif kind == "up":
                    _, c, f = t
                    copied(dve, p, ("gate", c, f))
                    v.scalar_tensor_tensor(out=hT[:, c, f, :], in0=bank, scalar=bu_sb[:, f:f + 1],
                                           in1=sgate[:, c, f, :], op0=ALU.add, op1=ALU.mult)\
                        .then_inc(ring_copied_vector, 1)
                elif kind == "max":
                    it, k0, w, heads = max_units(t[1])[t[2]]
                    v.tensor_reduce(pmax[:, it, k0 // CHUNK, heads[0]:heads[-1] + 1:2],
                                    bank[:, 0:w * len(heads)].rearrange("p (h w) -> p h w", w=w),
                                    axis=AX.X, op=ALU.max).then_inc(ring_copied_vector, 1)
                elif kind == "negate":
                    negated(p, t[1])

            def negated(p, st):
                c, half = st // 2, st % 2
                copied(dve, p, ("max", st, len(max_units(st)) - 1))
                hs = slice(half * H // 2, (half + 1) * H // 2)
                n = slice(c * TPC, (c + 1) * TPC)
                m = pmax[:, n, 0, hs]
                if c > 0:
                    k = steps.mark(v.tensor_tensor(mrest[:, :, :], m, pmax[:, n, 1, hs], ALU.max))
                    steps.need(k)
                    m = mrest[:, :, :]
                k = steps.mark(v.tensor_scalar(rmax[:, :, :], m, -1.0, None, ALU.mult))
                steps.need(k)
                filled_before(dve, p, ("negmaxT", st - 1) if st else None)
                pj = [ap.rearrange("p n (j e) -> p n e j", e=2) for ap in (rmax[:, :, :], mrest[:, :, :])]
                k = steps.mark(v.tensor_copy(negmax[:, :, :, 0, :], pj[0]))
                steps.need(k)
                k = steps.mark(v.tensor_tensor(pj[1], pj[0], negmax[:, :, :, 0, :], ALU.subtract))
                steps.need(k)
                k = steps.mark(v.tensor_copy(negmax[:, :, :, 1, :], pj[1]))
                steps.need(k)
                v.tensor_tensor(negmax[:, :, :, 2, :], pj[1], negmax[:, :, :, 1, :], ALU.subtract)\
                    .then_inc(negmax_ready, 1)

            def run(p):
                steps.begin(p)
                for phase, k, tasks in p.steps:
                    for t in tasks:
                        task(p, phase, t)
                steps.end(p)

            run(FIRST)
            with dve.Fori(0, B - 1) as i:
                run(loop_pass(i))
            run(LAST)

        @block.tensor
        def _(pe):
            t_ = nc.tensor
            pe.wait_ge(weights_loaded, 16 * NLOAD)
            pe.wait_ge(consts_made, NCONST)
            def setup_step(n):
                if n > 0:
                    pe.wait_ge(setup_copied, n)
                if n < NF:
                    ins = t_.transpose(sum_bank[:, 0:P], down_sb[:, n, :], ident[:, :])
                else:
                    h, k = (n - NF) // 4, (n - NF) % 4
                    if k == 0:
                        ins = t_.transpose(sum_bank[:, 0:P], wq_sb[:, h, :, :].rearrange("p a n -> p (a n)"),
                                           ident[:, :])
                    elif k == 1:
                        ins = t_.transpose(sum_bank[:, 0:NKEYS], keys_sb[:, h, :, :].rearrange("k a n -> k (a n)"),
                                           ident[0:NKEYS, 0:NKEYS])
                    else:
                        r = slice(HALF * (k - 2), HALF * (k - 1))
                        ins = t_.matmul(sum_bank[:, 0:NKEYS], wqT[r, :], keysT[r, :], start=True, stop=True)
                ins.then_inc(setup_filled, 1)

            for s in (ring_filled, sum_filled, scores_filled, probs_used):
                pe.sem_inc(s, START)
            def tokens(c):
                return slice(c * CHUNK, (c + 1) * CHUNK)

            def task(p, phase, t):
                kind, b = t[0], p.batch(phase, t)
                if kind in ("hidden", "out"):
                    c, e = t[1:]
                    last = next(u for u in SUMS if u[:2] == t[:2])
                    if e == 0:
                        pe.wait_ge(sum_read, START + b * NSUM + SUMS.index(last))
                    if t == ("hidden", 0, 0):
                        pe.wait_ge(ring_copied_vector, START + p.copy_base["vector"])
                    if kind == "hidden":
                        pair = (wd_sb[:, e, :], hT[:, c, e, :])
                    elif e == 0:
                        copied(pe, p, ("yT", c))
                        pair = (wproj_sb[:, :], yT[:, :])
                    else:
                        copied(pe, p, ("experts", c, e - 1))
                        pair = (up_sb[:, e - 1, :], gT[:, c, e - 1, :])
                    ins = t_.matmul(sum_bank[:, :], pair[0], pair[1], start=e == 0, stop=t == last)
                    if t == last:
                        ins.then_inc(sum_filled, 1)
                    return
                if t not in p.ring:
                    return
                n, bank = t[-1], bank_of(p, t)
                bankb = ringb[p.ring[t] % NRING]
                if p.ring[t] < NRING:
                    pe.wait_ge(ring_copied_scalar, START + p.copy_base["scalar"])
                    pe.wait_ge(ring_copied_vector, START + p.copy_base["vector"])
                else:
                    copied(pe, p, p.order[p.ring[t] - NRING])
                if kind == "qkv" and n % TPC == 0:
                    copied(pe, p, ("xT", n // TPC))
                if kind == "yT":
                    copied(pe, p, ("y", t[1], GROUPS - 1))
                if kind == "outT":
                    pe.wait_ge(sum_read, START + b * NSUM + SUMS.index(("out", t[1], NF)) + 1)
                if t == ("gate", 0, 0):
                    pe.wait_ge(xnT_moved, START + 16 * (b + 1))
                if t == ("max", 0, 0):
                    pe.wait_ge(parts_loaded, START + (b + 1) * (NSTACK * 16))
                if kind == "negmaxT":
                    pe.wait_ge(negmax_ready, START + b * STAGES_A + t[1] + 1)
                    for n in range(TPC):
                        ins = t_.transpose(bankb[:, n * P:(n + 1) * P], negmax_pad[:, n, :], identb[:, :])
                elif kind == "sim":
                    n = t[1]
                    ins = t_.matmul(bank, xnT[:, n * P:(n + 1) * P],
                                    wsim[:, :, :, :].rearrange("p a h k -> p (a h k)"), start=True, stop=True)
                elif kind == "down":
                    ins = t_.matmul(bank, downT[:, t[2] * P:(t[2] + 1) * P], xnT[:, tokens(t[1])],
                                    start=True, stop=True)
                elif kind == "y":
                    k = t[1] * GROUPS + t[2]
                    pe.wait_ge(yT4_ready, START + b * NC * GROUPS + k + 1)
                    for n in range(TPC):
                        ins = t_.transpose(bank[:, n * P:(n + 1) * P], yT4[:, n * P:(n + 1) * P], ident[:, :])
                elif kind == "yT":
                    for n in range(TPC):
                        ins = t_.transpose(bank[:, n * P:(n + 1) * P],
                                           ytm[:, n, :, :].rearrange("p h d -> p (h d)"), ident[:, :])
                elif kind == "experts":
                    pe.wait_ge(coef_ready, START + b * NT + (t[1] + 1) * TPC)
                    for n in range(TPC):
                        ins = t_.transpose(bank[:, n * P:(n + 1) * P], coef[:, n, t[2] * P:(t[2] + 1) * P],
                                           ident[:, :])
                elif kind == "outT":
                    for n in range(TPC):
                        ins = t_.transpose(bank[:, n * P:(n + 1) * P], oT[:, n * P:(n + 1) * P], ident[:, :])
                elif kind == "xT":
                    pe.wait_ge(xn_ready, START + b * NT + (n + 1) * TPC)
                    for m in range(TPC):
                        ins = t_.transpose(bank[:, m * P:(m + 1) * P], xn[:, n * TPC + m, :], ident[:, :])
                elif kind == "qkv":
                    ins = t_.matmul(bank[:, 0:3 * D], xnT_next[:, n * P:(n + 1) * P], wqkv_sb[:, :],
                                    start=True, stop=True)
                elif kind == "parts":
                    pe.wait_ge(parts_ready, START + b * NT + n + 1)
                    for a in range(2):
                        for s in range(3):
                            m = 3 * a + s
                            ins = t_.transpose(bankb[:, m * P:(m + 1) * P], parts[:, n % 2, s, a * D:(a + 1) * D],
                                               identb[:, :])
                elif kind in ("gate", "up"):
                    w = {"gate": wg_sb, "up": wu_sb}[kind]
                    ins = t_.matmul(bank, w[:, n * P:(n + 1) * P], xnT[:, tokens(t[1])], start=True, stop=True)
                elif kind == "max":
                    it, k0, w, heads = max_units(t[1])[n]
                    diag = k0 + w == P * (it + 1)
                    for s, h in enumerate(heads):
                        r = slice(HALF * (h % 2), HALF * (h % 2) + ROWS)
                        ins = t_.matmul(bank[:, s * w:(s + 1) * w], qs[r, h // 2, it * P:(it + 1) * P],
                                        ks[r, h // 2, k0:k0 + w], start=True, stop=not diag)
                        if diag:
                            ins = t_.matmul(bank[:, (s + 1) * w - P:(s + 1) * w], identb[:, :], mask_qk[:, :],
                                            start=False, stop=True)
                ins.then_inc(ring_filled, 1)

            def scores(i, n):
                _, gr, kt, h, q0 = EXP_UNITS[n]
                c = chunk_of(n)
                if n in STAGE_STARTS:
                    pe.wait_ge(negmax_loaded, START + (i * STAGES_A + STAGE_STARTS.index(n) + 1) * 2 * 16)
                pe.wait_ge(probs_ready, START + i * UNITS + max(n - NSB + 1, 0))
                r = slice(HALF * (h % 2), HALF * (h % 2) + ROWS)
                diag = kt >= c * TPC
                ins = t_.matmul(sbank[:, n % NSB, q0:CHUNK], ks[r, h // 2, kt * P:(kt + 1) * P],
                                qs[r, h // 2, c * CHUNK + q0:(c + 1) * CHUNK], start=True, stop=not diag)
                if diag:
                    ins = t_.matmul(sbank[:, n % NSB, q0:q0 + P], identb[:, :], mask_kq[:, :], start=False, stop=True)
                ins.then_inc(scores_filled, 1)

            def values(i, m):
                _, gr, kt, _, q0 = EXP_UNITS[4 * m]
                c = chunk_of(4 * m)
                pe.wait_ge(probs_ready, START + i * UNITS + 4 * (m + 1))
                if m == 0:
                    pe.wait_ge(v_moved, START + 16 * (i + 1))
                if kt == 0:
                    pe.wait_ge(yT4_ready, START + i * NC * GROUPS + c * GROUPS + gr)
                last = kt == (c + 1) * TPC - 1
                for j in range(4):
                    v0 = (4 * gr + j) * (DH + 1)
                    ins = t_.matmul(ybank[32 * j:32 * j + 32, q0:CHUNK], vaug[:, kt, v0:v0 + 32],
                                    pT[:, m % NPT, j, q0:CHUNK], start=kt == 0, stop=last)
                ins.then_inc(probs_used, 1)

            def run(p):
                for phase, k, tasks in p.steps:
                    if phase == "P" and p.i is not None:
                        scores(p.i, k)
                        if k % 4 == 1 and k >= 5:
                            values(p.i, k // 4 - 1)
                    for t in tasks:
                        task(p, phase, t)
                        if p is FIRST and phase == "P" and t in p.ring:
                            setup_step(p.ring[t])
                    if p is FIRST and phase == "P":
                        for n in range(len([t for t in tasks if t in p.ring]), len(SETUP)):
                            setup_step(n)
                        pe.wait_ge(setup_copied, len(SETUP))
                    if phase == "P" and p.i is not None and k == UNITS - 1:
                        values(p.i, PRODS - 1)

            run(FIRST)
            with pe.Fori(0, B - 1) as i:
                run(loop_pass(i))
            run(LAST)


_INS = ['L0_attn_x', 'L0_attn_Wqkv', 'L0_attn_Wproj', 'L0_ffn_Wg', 'L0_ffn_bg', 'L0_ffn_Wu', 'L0_ffn_bu', 'L0_ffn_Wd',
        'L0_ffn_bd', 'L0_ffn_Wq', 'L0_ffn_keys', 'L0_ffn_down_embed', 'L0_ffn_up_embed']


def rope_table():
    inv = np.float32(1.0) / np.float32(10000.0) ** (np.arange(0, DH, 2, dtype=np.float32) / np.float32(DH))
    angle = np.arange(T, dtype=np.float32)[:, None] * inv[None, :].astype(np.float32)
    cos = np.repeat(np.cos(angle), 2, axis=-1)
    sin = np.repeat(np.sin(angle), 2, axis=-1) * np.tile(np.array([-1.0, 1.0], np.float32), DH // 2)
    return np.stack([cos, sin]).astype(np.float32)


def kernel(**inputs):
    import concourse.bacc as bacc
    from concourse.bass_utils import run_bass_kernel_spmd

    nc = bacc.Bacc("TRN2", target_bir_lowering=False, num_devices=1)
    arrays = {f"in_{n}": np.ascontiguousarray(inputs[n]) for n in _INS}
    arrays["rope_table"] = rope_table()
    args = [nc.dram_tensor(n, a.shape, mybir.dt.from_np(a.dtype), kind="ExternalInput").ap()
            for n, a in arrays.items()]
    out = nc.dram_tensor("out_0", (B, T, D), F32, kind="ExternalOutput").ap()
    build(nc, *args, out)
    return run_bass_kernel_spmd(nc, [arrays], core_ids=[0]).results[0]["out_0"]
```
